# Optimizing a Trainium2 kernel written in Bass

```python
import numpy as np
import jax
import jax.numpy as jnp

def _softmax(x, axis=-1):
    return jax.nn.softmax(x, axis=axis)

def _gelu(x):
    return jax.nn.gelu(x, approximate=True)

def _silu(x):
    return jax.nn.silu(x)

def _sigmoid(x):
    return jax.nn.sigmoid(x)

def _layernorm(x, axis=-1, eps=1e-05):
    m = jnp.mean(x, axis=axis, keepdims=True)
    v = jnp.var(x, axis=axis, keepdims=True)
    return (x - m) / jnp.sqrt(v + eps)

def _scatter_add(tgt, idx, src, axis=0):
    return tgt.at[idx].add(src)

def _segment_sum(src, seg, n):
    return jax.ops.segment_sum(src, seg, n)
kernel_name = 'mk_gnn_resnorm_d1_gnn_r64_d28176'

def setup_inputs(seed: int=0):
    np.random.seed(seed)
    _w = jnp.asarray

    def _rec_inputs():
        import jax
        import jax.numpy as jnp
        _gk = jax.random.key(seed)
        x = -0.000202 + 1 * jax.random.normal(jax.random.fold_in(_gk, 1), (100000, 64), jnp.float32)
        src = jax.random.randint(jax.random.fold_in(_gk, 2), (50000,), 0, 100000, jnp.int32)
        dst = jnp.minimum((100000 * jax.random.uniform(jax.random.fold_in(_gk, 3), (50000,)) ** 2.0).astype(jnp.int32), 99999)
        _o = jnp.argsort(dst, stable=True)
        src = src[_o]
        dst = dst[_o]
        edge_attr_16 = -5.3897e-05 + 0.999841 * jax.random.normal(jax.random.fold_in(_gk, 12), (50000, 16), jnp.float32)
        return (x, src, dst, edge_attr_16)
    x, src, dst, edge_attr_16 = _rec_inputs()

    def _L0_gnn_setup():
        import jax, jax.numpy as jnp
        import numpy as np
        N_NODES = 100000
        N_EDGES = 25000
        D_IN = 64
        D_OUT = 64
        D_EDGE = 16
        NEG_SLOPE = 0.01
        LN_EPS = 1e-05
        key = jax.random.key(seed)
        ks = jax.random.split(key, 8)
        x = jax.random.normal(ks[0], (N_NODES, D_IN), dtype=jnp.float32)
        edge_attr = jax.random.normal(ks[1], (N_EDGES, D_EDGE), dtype=jnp.float32)
        W1 = jax.random.normal(ks[2], (D_OUT, D_IN + D_EDGE), dtype=jnp.float32) * 0.1
        W2 = jax.random.normal(ks[3], (D_OUT, D_IN), dtype=jnp.float32) * 0.1
        att_l = jax.random.normal(ks[4], (D_OUT,), dtype=jnp.float32) * 0.1
        att_r = jax.random.normal(ks[5], (D_IN,), dtype=jnp.float32) * 0.1
        bias = jnp.zeros((D_OUT,), dtype=jnp.float32)
        ln_gamma = jnp.ones((D_OUT,), dtype=jnp.float32)
        ln_beta = jnp.zeros((D_OUT,), dtype=jnp.float32)
        src = jax.random.randint(ks[6], (N_EDGES,), 0, N_NODES)
        dst = jax.random.randint(ks[7], (N_EDGES,), 0, N_NODES)
        return {'x': x, 'edge_attr': edge_attr, 'W1': W1, 'W2': W2, 'att_l': att_l, 'att_r': att_r, 'bias': bias, 'ln_gamma': ln_gamma, 'ln_beta': ln_beta, 'src': src, 'dst': dst}
    _L0_gnn_all = _L0_gnn_setup()
    _L0_gnn_in = {k: v for k, v in _L0_gnn_all.items() if k in ('W1', 'W2', 'att_l', 'att_r', 'bias', 'ln_gamma', 'ln_beta')}
    del _L0_gnn_all
    return {'x': x, 'src': src, 'dst': dst, 'edge_attr_16': edge_attr_16, 'L0_gnn_W1': _L0_gnn_in['W1'], 'L0_gnn_W2': _L0_gnn_in['W2'], 'L0_gnn_att_l': _L0_gnn_in['att_l'], 'L0_gnn_att_r': _L0_gnn_in['att_r'], 'L0_gnn_bias': _L0_gnn_in['bias'], 'L0_gnn_ln_gamma': _L0_gnn_in['ln_gamma'], 'L0_gnn_ln_beta': _L0_gnn_in['ln_beta']}

def reference(x, src, dst, edge_attr_16, L0_gnn_W1, L0_gnn_W2, L0_gnn_att_l, L0_gnn_att_r, L0_gnn_bias, L0_gnn_ln_gamma, L0_gnn_ln_beta):
    import jax
    import jax.numpy as jnp

    def _L0_gnn_ref(x, edge_attr, W1, W2, att_l, att_r, bias, ln_gamma, ln_beta, src, dst):
        import jax, jax.numpy as jnp
        import numpy as np
        N_NODES = 100000
        N_EDGES = 25000
        D_IN = 64
        D_OUT = 64
        D_EDGE = 16
        NEG_SLOPE = 0.01
        LN_EPS = 1e-05
        N = x.shape[0]
        x_t = x @ W2.T
        ar = (x * att_r).sum(-1)
        er = ar[dst]
        f_srt = jnp.concatenate([x[src], edge_attr], axis=-1) @ W1.T
        el = (f_srt * att_l).sum(-1)
        e = jax.nn.leaky_relu(er + el, NEG_SLOPE)
        e_max = jax.ops.segment_max(e, dst, num_segments=N)
        ex = jnp.exp(e - e_max[dst])
        denom = jax.ops.segment_sum(ex, dst, num_segments=N)
        alpha = ex / denom[dst]
        m = x_t[src] * alpha[:, None]
        h = jax.ops.segment_sum(m, dst, num_segments=N)
        out = h + bias
        mu = out.mean(-1, keepdims=True)
        var = ((out - mu) ** 2).mean(-1, keepdims=True)
        out = (out - mu) * jax.lax.rsqrt(var + LN_EPS) * ln_gamma + ln_beta
        return out
    x = _layernorm(x + _L0_gnn_ref(x, edge_attr_16, L0_gnn_W1, L0_gnn_W2, L0_gnn_att_l, L0_gnn_att_r, L0_gnn_bias, L0_gnn_ln_gamma, L0_gnn_ln_beta, src, dst), axis=-1)
    return x

_drawn_inputs = setup_inputs


def setup_inputs(seed=0):
    import zlib

    import numpy as np

    out = dict(_drawn_inputs(seed))
    spreads = {'L0_gnn_bias': (0.0, 0.1), 'L0_gnn_ln_gamma': (1.0, 0.2), 'L0_gnn_ln_beta': (0.0, 0.1)}
    factors = {}
    for name, (base, spread) in spreads.items():
        noise = np.random.default_rng([zlib.crc32(name.encode()), seed]).standard_normal(out[name].shape)
        drawn = base * np.exp(spread * noise) if base else spread * noise
        out[name] = jnp.asarray(drawn.astype(out[name].dtype))
    for name, factor in factors.items():
        out[name] = (out[name] * factor).astype(out[name].dtype)
    return out
```

```python
import concourse.bass as bass
from concourse import mybir
from contextlib import ExitStack


def gnn_resnorm(nc, x, src, dst, edge_attr, W1, W2, att_l, att_r, bias, gamma, beta, out):
    f32, i32 = mybir.dt.float32, mybir.dt.int32
    ALU, ACT, AX = mybir.AluOpType, mybir.ActivationFunctionType, mybir.AxisListType.X

    P = 128
    NODES, D = x.shape
    EDGES, DE = edge_attr.shape
    GC = 14
    GROUPS = 28
    COLS = GC * GROUPS
    FULLP = EDGES // COLS
    REST = EDGES - FULLP * COLS
    assert FULLP == P - 1 and 0 < REST <= COLS
    J = 28
    BLOCKS = GROUPS
    LASTN = NODES - (BLOCKS - 1) * P * J
    LJ = 32
    LP = LASTN // LJ
    assert LP * LJ == LASTN and LP <= P
    JM = max(J, LJ)
    H = GC // 2
    E1 = D + 1
    EPS, SLOPE = 1e-5, 0.01
    BIG = 1e30
    FD = 40
    FAR = 1 << 20

    spill = nc.dram_tensor("xdst_rows", (P, COLS * D), f32).ap()

    def dense(t, b, last):
        if last:
            return t[(BLOCKS - 1) * P * J:NODES, :].rearrange("(p j) f -> p j f", p=LP)
        return t[bass.ds(b * (P * J), P * J), :].rearrange("(p j) f -> p j f", p=P)

    def group(t, g, n=GC):
        return t[:, bass.ds(g * n, n)]

    ctx = ExitStack()
    with ctx:
        def sb(name, shape, dt=f32):
            return ctx.enter_context(nc.sbuf_tensor(name, shape, dt))

        def sem(name):
            return ctx.enter_context(nc.semaphore(name))

        def pair(name):
            return [sem(f"{name}{b}") for b in range(2)]

        ident = sb("ident", [P, P])
        ones = sb("ones", [P, P])
        eps = sb("eps", [P, 1])
        later = sb("later", [P, P])
        w1 = sb("w1", [D, D + DE])
        w2 = sb("w2", [D, 2 * D])
        w1d = sb("w1d", [D, 2 * D])
        centre = sb("centre", [D, D])
        al = sb("al", [D, 1])
        alrep = sb("alrep", [D, P])
        rows = sb("rows", [P, 4, D])
        arow, brow, grow, erow = (rows[:, k, :] for k in range(4))
        vrow = sb("vrow", [P, D + DE])
        wc = sb("wc", [P, E1])
        brep = sb("brep", [P, H, E1])
        crow = sb("crow", [P, D])
        sc = sb("sc", [P, 8])
        srci = sb("srci", [P, COLS], i32)
        dsti = sb("dsti", [P, COLS], i32)
        dstg = sb("dstg", [P, COLS], i32)
        nxti = sb("nxti", [P, 1], i32)
        dstf = sb("dstf", [P, COLS])
        nxtf = sb("nxtf", [P, 1])
        el = sb("el", [P, COLS])
        er = sb("er", [P, COLS])
        s0 = sb("s0", [P, COLS])
        s1 = sb("s1", [P, COLS])
        pen = sb("pen", [P, COLS + 1])
        same = sb("same", [P, COLS + 1])
        isfirst = sb("isfirst", [P, COLS])
        scat = sb("scat", [P, COLS], i32)
        xt = sb("xt", [P, COLS, E1])
        idx = [sb(f"idx{b}", [P, 2, GC], i32) for b in range(2)]
        xs = [sb(f"xs{b}", [P, GC, D]) for b in range(2)]
        xd = [sb(f"xd{b}", [P, GC, D]) for b in range(2)]
        xsT = [sb(f"xsT{b}", [P, H, P]) for b in range(2)]
        xin = [sb(f"xin{b}", [P, JM, D]) for b in range(2)]
        yb = [sb(f"yb{b}", [P, JM, D]) for b in range(2)]
        work = sb("work", [P, GC, D])
        sq = sb("sq", [P, JM, D])
        st = sb("st", [P, 4, JM])
        tails = sb("tails", [P, 4, P])
        cand = sb("cand", [P, 2, P])
        gmax = sb("gmax", [P, 4])
        reach = sb("reach", [P, P])
        carry = sb("carry", [P, E1])

        psT = [ctx.enter_context(nc.psum_tensor(f"psT{b}", [P, 2, 512], f32)) for b in range(2)]
        psX = [ctx.enter_context(nc.psum_tensor(f"psX{b}", [P, 2, 512], f32)) for b in range(2)]

        s_const = sem("s_const")
        s_pads = sem("s_pads")
        s_load = sem("s_load")
        s_edge = sem("s_edge")
        s_attr = sem("s_attr")
        s_alrep = sem("s_alrep")
        s_wps = sem("s_wps")
        s_wsb = sem("s_wsb")
        s_attru = sem("s_attru")
        s_idx = pair("s_idx")
        s_gs = pair("s_gs")
        s_gd = pair("s_gd")
        s_tr = pair("s_tr")
        s_tc = pair("s_tc")
        s_xm = pair("s_xm")
        s_xc = pair("s_xc")
        s_er = pair("s_er")
        s_sp = pair("s_sp")
        s_xin = pair("s_xin")
        s_xu = pair("s_xu")
        s_yc = pair("s_yc")
        s_sq = pair("s_sq")
        s_y = pair("s_y")
        s_st = pair("s_st")
        s_var = pair("s_var")
        s_dev = pair("s_dev")
        s_bv = sem("s_bv")
        s_bd = sem("s_bd")
        s_v = sem("s_v")
        s_e = sem("s_e")
        s_ex = sem("s_ex")
        s_tail = sem("s_tail")
        s_tps = sem("s_tps")
        s_mul = sem("s_mul")
        s_run = sem("s_run")
        s_cps = sem("s_cps")
        s_re = pair("s_re")
        s_a = pair("s_a")
        s_asq = pair("s_asq")
        s_b = pair("s_b")
        s_bsq = pair("s_bsq")
        s_av = pair("s_av")
        s_ad = pair("s_ad")
        s_bvar = pair("s_bvar")
        s_bdev = pair("s_bdev")
        s_z = pair("s_z")
        s_sc = pair("s_sc")

        attr = xt[:, :, :].rearrange("p c f -> p (c f)")[:, 0:COLS * DE].rearrange("p (c f) -> p c f", f=DE)

        block = ctx.enter_context(nc.Block())

        class Steps:
            base, n = 0, 0

            def __call__(self, ins):
                ins.then_inc(s_v, 1)
                self.n += 1
                nc.vector.wait_ge(s_v, self.base + self.n)

        def wait_free(eng, s, count):
            if not (isinstance(count, int) and count == 0):
                eng.wait_ge(s, count)

        def sums_of(b):
            return xin[b][:, 0:GC, :]

        def over(row, n, width=D):
            return row.unsqueeze(1).broadcast_to([row.shape[0], n, width])

        def along(cols, width=D):
            return cols.unsqueeze(2).broadcast_to([cols.shape[0], cols.shape[1], width])

        @block.sync
        def _(sp):
            sp.dma_start(w1[:, :], W1).then_inc(s_load, 16)
            for k in range(2):
                sp.dma_start(w2[:, k * D:(k + 1) * D], W2).then_inc(s_load, 16)
                sp.dma_start(w1d[:, k * D:(k + 1) * D], W1[:, 0:D]).then_inc(s_load, 16)
            with nc.allow_non_contiguous_dma(reason="one number for each partition"):
                sp.dma_start(al[:, :], att_l.unsqueeze(1)).then_inc(s_load, 16)
            for k, row in enumerate((att_r, bias, gamma, beta)):
                sp.dma_start(rows[:, k, :], row.unsqueeze(0).broadcast_to([P, D])).then_inc(s_load, 16)
            sp.wait_ge(s_pads, 1)
            for to, a in ((srci, src), (dstg, dst), (dsti, dst)):
                sp.dma_start(to[0:FULLP, :],
                             a[0:FULLP * COLS].rearrange("(p c) -> p c", p=FULLP)).then_inc(s_edge, 16)
                sp.dma_start(to[FULLP:P, 0:REST],
                             a[FULLP * COLS:EDGES].rearrange("(p c) -> p c", p=1)).then_inc(s_edge, 16)
            with nc.allow_non_contiguous_dma(reason="one number for each partition"):
                sp.dma_start(nxti[0:FULLP, :], dst.unsqueeze(1)[COLS:EDGES:COLS, :]).then_inc(s_edge, 16)
            sp.dma_start(attr[0:FULLP], edge_attr[0:FULLP * COLS, :].rearrange("(p c) f -> p c f", p=FULLP)
                         ).then_inc(s_attr, 16)
            sp.dma_start(attr[FULLP:P, 0:REST, :], edge_attr[FULLP * COLS:EDGES, :].rearrange("(p c) f -> p c f", p=1)
                         ).then_inc(s_attr, 16)
            for b in range(2):
                sp.dma_start(xin[b][:, 0:J, :], dense(x, b, False)).then_inc(s_xin[b], 16)

            def stores(i, last):
                for b in range(2):
                    g = i * 2 + b
                    end = last and b == 1
                    np_, nj = (LP, LJ) if end else (P, J)
                    if not last:
                        sp.wait_ge(s_xu[b], i + 1)
                        sp.dma_start(xin[b][:, 0:J, :], dense(x, g + 2, False)).then_inc(s_xin[b], 16)
                    sp.wait_ge(s_er[b], i + 1)
                    sp.dma_start(group(spill, g, GC * D), xd[b][:, :, :].rearrange("p c f -> p (c f)")
                                 ).then_inc(s_sp[b], 16)
                    sp.wait_ge(s_y[b], i + 1)
                    sp.dma_start(dense(out, g, end), yb[b][0:np_, 0:nj, :]).then_inc(s_st[b], 16)

            pairs = GROUPS // 2
            with sp.Fori(0, pairs - 2) as i:
                stores(i, False)
            i = pairs - 2
            for b in range(2):
                sp.wait_ge(s_xu[b], i + 1)
                np_, nj = (LP, LJ) if b else (P, J)
                sp.dma_start(xin[b][0:np_, 0:nj, :], dense(x, 2 * i + b + 2, b == 1)).then_inc(s_xin[b], 16)
                sp.wait_ge(s_er[b], i + 1)
                sp.dma_start(group(spill, 2 * i + b, GC * D), xd[b][:, :, :].rearrange("p c f -> p (c f)")
                             ).then_inc(s_sp[b], 16)
                sp.wait_ge(s_y[b], i + 1)
                sp.dma_start(dense(out, 2 * i + b, False), yb[b][:, 0:J, :]).then_inc(s_st[b], 16)
            stores(pairs - 1, True)

            for b in range(2):
                sp.wait_ge(s_sp[b], 16 * pairs)
            for b in range(2):
                sp.dma_start(xd[b][:, :, :].rearrange("p c f -> p (c f)"), group(spill, b, GC * D)
                             ).then_inc(s_re[b], 16)
            with sp.Fori(0, pairs - 1) as i:
                for b in range(2):
                    sp.wait_ge(s_b[b], i + 1)
                    sp.dma_start(xd[b][:, :, :].rearrange("p c f -> p (c f)"), group(spill, i * 2 + b + 2, GC * D)
                                 ).then_inc(s_re[b], 16)
            for b in range(2):
                sp.wait_ge(s_st[b], 16 * pairs)

        @block.gpsimd
        def _(pool):
            nc.gpsimd.memset(srci[:, :], 0)
            nc.gpsimd.memset(dstg[:, :], 0)
            nc.gpsimd.memset(dsti[:, :], FAR)
            nc.gpsimd.memset(attr, 0.0)
            nc.gpsimd.memset(nxti[:, :], 2 * FAR).then_inc(s_pads, 1)
            nc.gpsimd.memset(ident[:, :], 0.0)
            nc.gpsimd.memset(ones[:, :], 1.0)
            nc.gpsimd.memset(eps[:, :], EPS)
            nc.gpsimd.memset(centre[:, :], -1.0 / D).then_inc(s_const, 1)
            pool.wait_ge(s_const, 1)
            nc.gpsimd.affine_select(out=ident[:, :], in_=ident[:, :], compare_op=ALU.not_equal, fill=1.0,
                                    base=0, pattern=[[1, P]], channel_multiplier=-1)
            nc.gpsimd.affine_select(out=later[:, :], in_=ones[:, :], compare_op=ALU.is_gt, fill=0.0,
                                    base=0, pattern=[[1, P]], channel_multiplier=-1)
            nc.gpsimd.affine_select(out=centre[:, :], in_=centre[:, :], compare_op=ALU.not_equal, fill=1.0 - 1.0 / D,
                                    base=0, pattern=[[1, D]], channel_multiplier=-1).then_inc(s_const, 1)

            def gathers(i):
                first = isinstance(i, int)
                before, after, spilled = (i, i + 1, i * 16) if first else (
                    i, pool.to_reg(i + 1), pool.to_reg(i * 16))
                for b in range(2):
                    pool.wait_ge(s_const, 1)
                    pool.wait_ge(s_idx[b], after)
                    wait_free(pool, s_tr[b], before)
                    for k in range(GC):
                        nc.gpsimd.indirect_dma_start(xs[b][:, k, :], None, x[:, :], bass.IndirectOffsetOnAxis(
                            ap=idx[b][:, 0, k:k + 1], axis=0)).then_inc(s_gs[b], 16)
                    pool.wait_ge(s_const, 1)
                    wait_free(pool, s_sp[b], spilled)
                    for k in range(GC):
                        nc.gpsimd.indirect_dma_start(xd[b][:, k, :], None, x[:, :], bass.IndirectOffsetOnAxis(
                            ap=idx[b][:, 1, k:k + 1], axis=0)).then_inc(s_gd[b], 16)

            gathers(0)
            with pool.Fori(1, GROUPS // 2) as i:
                gathers(i)

            pool.wait_ge(s_ex, 1)
            nc.gpsimd.tensor_tensor(xt[:, :, FD:D], xt[:, :, FD:D], along(xt[:, :, D], D - FD), ALU.mult
                                    ).then_inc(s_mul, 1)
            for b in range(2):
                pool.wait_ge(s_st[b], 16 * (GROUPS // 2))
            with pool.Fori(0, GROUPS // 2) as i:
                after = pool.to_reg(i + 1)
                for b in range(2):
                    pool.wait_ge(s_const, 1)
                    pool.wait_ge(s_z[b], after)
                    for k in range(GC):
                        nc.gpsimd.indirect_dma_start(out[:, :], bass.IndirectOffsetOnAxis(
                            ap=idx[b][:, 0, k:k + 1], axis=0), yb[b][:, k, :], None,
                            bounds_check=NODES - 1, oob_is_err=False).then_inc(s_sc[b], 16)
            for b in range(2):
                pool.wait_ge(s_sc[b], 16 * GC * (GROUPS // 2))

        @block.scalar
        def _(act):
            def deviation(total):
                return nc.scalar.activation(total, total, ACT.Sqrt, scale=1.0 / D, bias=eps[0:total.shape[0], :])

            act.wait_ge(s_const, 1)
            act.wait_ge(s_bv, 1)
            deviation(sc[:, 1:2]).then_inc(s_bd, 1)

            def part(i, last):
                for b in range(2):
                    np_, nj = (LP, LJ) if last and b == 1 else (P, J)
                    act.wait_ge(s_tr[b], i + 1)
                    wait_free(act, s_xm[b], i)
                    nc.scalar.copy(xsT[b][:, 0:4, :].rearrange("p k e -> p (k e)"), psT[b][:, 0, :])
                    nc.scalar.copy(xsT[b][:, 4:H, :].rearrange("p k e -> p (k e)"), psT[b][:, 1, 0:(H - 4) * P]
                                   ).then_inc(s_tc[b], 1)
                    act.wait_ge(s_yc[b], i + 1)
                    nc.scalar.activation(sq[0:np_, 0:nj, :], yb[b][0:np_, 0:nj, :], ACT.Square).then_inc(s_sq[b], 1)
                    act.wait_ge(s_var[b], i + 1)
                    deviation(st[0:np_, 1, 0:nj]).then_inc(s_dev[b], 1)
                    act.wait_ge(s_xm[b], i + 1)
                    for h in range(2):
                        last_copy = nc.scalar.copy(
                            xt[:, bass.ds(i * (2 * GC) + b * GC, GC), :].rearrange("p (k h) f -> p k h f", h=2)[:, :, h, :],
                            psX[b][:, h, 0:H * E1].rearrange("p (k f) -> p k f", f=E1))
                    last_copy.then_inc(s_xc[b], 1)

            act.wait_ge(s_attru, 1)
            part(0, False)
            with act.Fori(1, GROUPS // 2 - 1) as i:
                part(i, False)
            part(GROUPS // 2 - 1, True)
            act.wait_ge(s_e, 1)
            nc.scalar.activation(xt[:, :, D], s0[:, :], ACT.Exp).then_inc(s_ex, 1)
            with act.Fori(0, GROUPS // 2) as i:
                for b in range(2):
                    act.wait_ge(s_a[b], i + 1)
                    nc.scalar.activation(sq[:, 0:GC, :], sums_of(b), ACT.Square).then_inc(s_asq[b], 1)
                    act.wait_ge(s_av[b], i + 1)
                    deviation(st[:, 1, 0:GC]).then_inc(s_ad[b], 1)
                    act.wait_ge(s_b[b], i + 1)
                    nc.scalar.activation(sq[:, 0:GC, :], yb[b][:, 0:GC, :], ACT.Square).then_inc(s_bsq[b], 1)
                    act.wait_ge(s_bvar[b], i + 1)
                    deviation(st[:, 3, 0:GC]).then_inc(s_bdev[b], 1)

        @block.tensor
        def _(pe):
            pe.wait_ge(s_load, 16 * 10)
            pe.wait_ge(s_alrep, 1)
            nc.tensor.matmul(psT[0][:, 0, 0:D + DE], alrep[:, :], w1[:, :], start=True, stop=True)
            nc.tensor.matmul(psT[0][:, 1, 0:D], w2[:, :], centre[:, :], start=True, stop=True)
            nc.tensor.matmul(psT[1][:, 0, 0:1], w1d[:, :], al[:, :], start=True, stop=True).then_inc(s_wps, 1)
            pe.wait_ge(s_wsb, 1)

            def products(i):
                for b in range(2):
                    pe.wait_ge(s_gs[b], i * (16 * GC) + 16 * GC)
                    wait_free(pe, s_tc[b], i)
                    for k in range(H):
                        last = nc.tensor.transpose(psT[b][:, k // 4, (k % 4) * P:(k % 4 + 1) * P],
                                                   xs[b][:, 2 * k:2 * k + 2, :].rearrange("p c f -> p (c f)"),
                                                   ident[:, :])
                    last.then_inc(s_tr[b], 1)
                    pe.wait_ge(s_tc[b], i + 1)
                    wait_free(pe, s_xc[b], i)
                    for h in range(2):
                        half = slice(D * h, D * (h + 1))
                        nc.tensor.matmul(psX[b][:, h, 0:H * E1], ones[half, :],
                                         brep[half, :, :].rearrange("p c f -> p (c f)"), start=True, stop=False)
                        for k in range(H):
                            last = nc.tensor.matmul(psX[b][:, h, k * E1:(k + 1) * E1], xsT[b][half, k, :],
                                                    wc[half, :], start=False, stop=(k == H - 1))
                    last.then_inc(s_xm[b], 1)

            products(0)
            with pe.Fori(1, GROUPS // 2) as i:
                products(i)
            pe.wait_ge(s_tail, 1)
            for b in range(2):
                pe.wait_ge(s_tc[b], GROUPS // 2)
            nc.tensor.matmul(psT[0][:, 0, :], ones[:, :], tails[:, :, :].rearrange("p k q -> p (k q)"),
                             start=True, stop=True).then_inc(s_tps, 1)
            pe.wait_ge(s_run, 1)
            nc.tensor.matmul(psX[0][:, 0, 0:E1], reach[:, :], xt[:, COLS - 1, :], start=True, stop=True
                             ).then_inc(s_cps, 1)

        @block.vector
        def _(dve):
            V = nc.vector
            step = Steps()

            def done(ins, s, count):
                ins.then_inc(s, 1)
                dve.wait_ge(s, count)

            def copy_idx(g, b):
                V.tensor_copy(idx[b][:, 0, :], group(srci, g))
                V.tensor_copy(idx[b][:, 1, :], group(dstg, g)).then_inc(s_idx[b], 1)

            dve.wait_ge(s_edge, 16 * 7)
            for b in range(2):
                copy_idx(b, b)
            dve.wait_ge(s_load, 16 * 10)
            dve.wait_ge(s_const, 2)
            V.tensor_copy(alrep[:, :], al[:, 0:1].broadcast_to([D, P])).then_inc(s_alrep, 1)
            step(V.tensor_reduce(sc[:, 0:1], brow, AX, ALU.add))
            step(V.tensor_scalar(sc[:, 0:1], sc[:, 0:1], 1.0 / D, None, ALU.mult))
            step(V.tensor_scalar(brow, brow, sc[:, 0:1], None, ALU.subtract))
            step(V.tensor_tensor(crow[:, :], brow, brow, ALU.mult))
            V.tensor_reduce(sc[:, 1:2], crow[:, :], AX, ALU.add).then_inc(s_bv, 1)
            dve.wait_ge(s_bd, 1)
            step(V.reciprocal(sc[:, 2:3], sc[:, 1:2]))
            step(V.tensor_scalar(crow[:, :], brow, sc[:, 2:3], None, ALU.mult))
            step(V.tensor_tensor(crow[:, :], crow[:, :], grow, ALU.mult))
            step(V.tensor_tensor(crow[:, :], crow[:, :], erow, ALU.add))
            step(V.memset(brep[:, :, :], 0.0))
            step(V.tensor_scalar(brep[:, :, 0:D], over(brow, H), 1.0 / D, None, ALU.mult))
            dve.wait_ge(s_wps, 1)
            step(V.tensor_copy(vrow[:, :], psT[0][:, 0, 0:D + DE]))
            step(V.tensor_copy(wc[:, 0:D], psT[0][:, 1, 0:D]))
            done(V.tensor_copy(wc[:, D:E1], psT[1][:, 0, 0:1]), s_wsb, 1)
            dve.wait_ge(s_attr, 32)
            step(V.tensor_tensor(attr, attr, over(vrow[:, D:D + DE], COLS, DE), ALU.mult))
            done(V.tensor_reduce(el[:, :], attr, AX, ALU.add), s_attru, 1)

            def part(i, last):
                for b in range(2):
                    g = i * 2 + b
                    np_, nj = (LP, LJ) if last and b == 1 else (P, J)
                    y, q, t = yb[b][0:np_, 0:nj, :], sq[0:np_, 0:nj, :], st[0:np_, :, 0:nj]
                    dve.wait_ge(s_xin[b], i * 16 + 16)
                    wait_free(dve, s_st[b], i * 16)
                    done(V.tensor_tensor(y, xin[b][0:np_, 0:nj, :], over(crow[0:np_, :], nj), ALU.add), s_xu[b], i + 1)
                    step(V.tensor_reduce(t[:, 0, :], y, AX, ALU.add))
                    step(V.tensor_scalar(t[:, 0, :], t[:, 0, :], 1.0 / D, None, ALU.mult))
                    done(V.tensor_tensor(y, y, along(t[:, 0, :]), ALU.subtract), s_yc[b], i + 1)
                    dve.wait_ge(s_gs[b], i * (16 * GC) + 16 * GC)
                    dve.wait_ge(s_gd[b], i * (16 * GC) + 16 * GC)
                    if not last:
                        copy_idx(g + 2, b)
                    step(V.tensor_tensor(work[:, :, :], xd[b][:, :, :], over(arow, GC), ALU.mult))
                    dve.wait_ge(s_sq[b], i + 1)
                    V.tensor_reduce(t[:, 1, :], q, AX, ALU.add).then_inc(s_var[b], 1)
                    step(V.tensor_reduce(group(er, g), work[:, :, :], AX, ALU.add))
                    V.tensor_tensor(xd[b][:, :, :], xd[b][:, :, :], over(erow, GC), ALU.add).then_inc(s_er[b], 1)
                    dve.wait_ge(s_dev[b], i + 1)
                    step(V.reciprocal(t[:, 1, :], t[:, 1, :]))
                    V.tensor_tensor(y, y, along(t[:, 1, :]), ALU.mult).then_inc(s_y[b], 1)

            def repeat(count, body):
                start = step.n
                body(0)
                assert step.n == start + PER[body.__name__], (body.__name__, step.n - start)
                with dve.Fori(1, count) as i:
                    step.base, step.n = i * PER[body.__name__] + start, 0
                    body(i)
                step.base, step.n = 0, start + count * PER[body.__name__]

            PER = {"dense_and_er": 2 * 5, "rows_out": 2 * 14}

            def dense_and_er(i):
                part(i, False)

            repeat(GROUPS // 2 - 1, dense_and_er)
            part(GROUPS // 2 - 1, True)

            dfirst, dlast = dstf[:, 0:1], dstf[:, COLS - 1:COLS]
            V.tensor_copy(nxtf[:, :], nxti[:, :])
            V.memset(same[:, 0:1], 0.0)
            step(V.tensor_copy(dstf[:, :], dsti[:, :]))
            V.tensor_tensor(same[:, 1:COLS], dstf[:, 1:COLS], dstf[:, 0:COLS - 1], ALU.is_equal)
            step(V.tensor_tensor(same[:, COLS:COLS + 1], dlast, nxtf[:, :], ALU.is_equal))
            V.tensor_scalar(pen[:, :], same[:, :], 1.0, BIG, ALU.subtract, ALU.mult)
            V.tensor_scalar(isfirst[:, :], dstf[:, :], dfirst, None, ALU.is_equal)
            step(V.scalar_tensor_tensor(s1[:, :], same[:, 1:COLS + 1], float(FAR), dstf[:, :], ALU.mult, ALU.add))
            V.tensor_copy(scat[:, :], s1[:, :])
            for b in range(2):
                dve.wait_ge(s_xc[b], GROUPS // 2)
            step(V.tensor_tensor(el[:, :], el[:, :], xt[:, :, D], ALU.add))
            step(V.tensor_tensor(er[:, :], er[:, :], el[:, :], ALU.add))
            step(V.scalar_tensor_tensor(er[:, :], er[:, :], SLOPE, er[:, :], ALU.mult, ALU.max))
            step(V.tensor_tensor_scan(s0[:, :], pen[:, 0:COLS], er[:, :], -BIG, ALU.add, ALU.max))
            step(V.tensor_tensor_scan(el[:, ::-1], pen[:, COLS:0:-1], s0[:, ::-1], -BIG, ALU.add, ALU.max))
            for k, end in enumerate((dlast, dfirst, s0[:, COLS - 1:COLS], el[:, 0:1])):
                ins = V.tensor_scalar(tails[:, k, :], ident[:, :], end, None, ALU.mult)
            ins.then_inc(s_tail, 1)
            dve.wait_ge(s_tps, 1)
            ends = psT[0][:, 0, :].rearrange("p (k q) -> p k q", q=P)
            for k, end in enumerate((dfirst, dlast)):
                step(V.tensor_scalar(cand[:, :, :], ends[:, 0:2, :], end, -BIG, ALU.not_equal, ALU.mult))
                step(V.tensor_tensor(cand[:, :, :], cand[:, :, :], ends[:, 2:4, :], ALU.add))
                step(V.tensor_reduce(gmax[:, k:k + 1], cand[:, :, :].rearrange("p k q -> p (k q)"), AX, ALU.max))
                step(V.tensor_scalar(s0[:, :], dstf[:, :], end, -BIG, ALU.not_equal, ALU.mult))
                step(V.scalar_tensor_tensor(el[:, :], s0[:, :], gmax[:, k:k + 1], el[:, :], ALU.add, ALU.max))
            V.tensor_tensor(s0[:, :], er[:, :], el[:, :], ALU.subtract).then_inc(s_e, 1)
            step(V.scalar_tensor_tensor(reach[:, :], ends[:, 1, :], dlast, later[:, :], ALU.is_equal, ALU.mult))

            dve.wait_ge(s_ex, 1)
            step(V.tensor_tensor(xt[:, :, 0:FD], xt[:, :, 0:FD], along(xt[:, :, D], FD), ALU.mult))
            for f in range(FD):
                V.tensor_tensor_scan(xt[:, :, f], same[:, 0:COLS], xt[:, :, f], 0.0, ALU.mult, ALU.add)
            dve.wait_ge(s_mul, 1)
            for f in range(FD, E1):
                ins = V.tensor_tensor_scan(xt[:, :, f], same[:, 0:COLS], xt[:, :, f], 0.0, ALU.mult, ALU.add)
            done(ins, s_run, 1)
            dve.wait_ge(s_cps, 1)
            step(V.tensor_copy(carry[:, :], psX[0][:, 0, 0:E1]))

            for b in range(2):
                dve.wait_ge(s_st[b], 16 * (GROUPS // 2))

            def rows_out(i):
                for b in range(2):
                    g = i * 2 + b
                    a = sums_of(b)
                    y, q = yb[b][:, 0:GC, :], sq[:, 0:GC, :]
                    den, rs, mu, dv = (st[:, k, 0:GC] for k in range(4))
                    first = group(isfirst, g)
                    sums = xt[:, bass.ds(g * GC, GC), :]
                    step(V.tensor_tensor(work[:, :, :], along(first), over(carry[:, 0:D], GC), ALU.mult))
                    V.tensor_tensor(a, sums[:, :, 0:D], work[:, :, :], ALU.add).then_inc(s_a[b], 1)
                    step(V.scalar_tensor_tensor(den, first, carry[:, D:E1], sums[:, :, D], ALU.mult, ALU.add))
                    step(V.tensor_scalar(den, den, 1e-30, None, ALU.max))
                    step(V.reciprocal(den, den))
                    dve.wait_ge(s_asq[b], i + 1)
                    step(V.tensor_reduce(rs, q, AX, ALU.add))
                    step(V.tensor_tensor(rs, rs, den, ALU.mult))
                    V.tensor_tensor(rs, rs, den, ALU.mult).then_inc(s_av[b], 1)
                    dve.wait_ge(s_ad[b], i + 1)
                    step(V.reciprocal(rs, rs))
                    step(V.tensor_tensor(rs, rs, den, ALU.mult))
                    wait_free(dve, s_sc[b], i * (16 * GC))
                    V.tensor_copy(idx[b][:, 0, :], group(scat, g))
                    step(V.tensor_tensor(y, a, along(rs), ALU.mult))
                    step(V.tensor_tensor(y, y, over(grow, GC), ALU.mult))
                    dve.wait_ge(s_re[b], i * 16 + 16)
                    step(V.tensor_tensor(y, y, xd[b][:, :, :], ALU.add))
                    step(V.tensor_reduce(mu, y, AX, ALU.add))
                    step(V.tensor_scalar(mu, mu, 1.0 / D, None, ALU.mult))
                    done(V.tensor_tensor(y, y, along(mu), ALU.subtract), s_b[b], i + 1)
                    dve.wait_ge(s_bsq[b], i + 1)
                    V.tensor_reduce(dv, q, AX, ALU.add).then_inc(s_bvar[b], 1)
                    dve.wait_ge(s_bdev[b], i + 1)
                    step(V.reciprocal(dv, dv))
                    V.tensor_tensor(y, y, along(dv), ALU.mult).then_inc(s_z[b], 1)

            repeat(GROUPS // 2, rows_out)


def kernel(**inputs):
    import numpy as _np
    import concourse.bacc as _bacc
    from concourse import mybir as _mybir
    from concourse.bass_utils import run_bass_kernel_spmd as _run

    nc = _bacc.Bacc("TRN2", target_bir_lowering=False, num_devices=1)
    arrays, args = {}, []
    for name in ("x", "src", "dst", "edge_attr_16", "L0_gnn_W1", "L0_gnn_W2", "L0_gnn_att_l", "L0_gnn_att_r",
                 "L0_gnn_bias", "L0_gnn_ln_gamma", "L0_gnn_ln_beta"):
        a = _np.ascontiguousarray(inputs[name])
        arrays[f"in_{name}_dram"] = a
        args.append(nc.dram_tensor(f"in_{name}_dram", a.shape, _mybir.dt.from_np(a.dtype), kind="ExternalInput").ap())
    args.append(nc.dram_tensor("out_0_dram", (100000, 64), _mybir.dt.float32, kind="ExternalOutput").ap())
    gnn_resnorm(nc, *args)
    r = _run(nc, [arrays], core_ids=[0])
    return r.results[0]["out_0_dram"]
```

```python
import concourse.bass as bass
from concourse import mybir
from contextlib import ExitStack


def gnn_resnorm(nc, x, src, dst, edge_attr, W1, W2, att_l, att_r, bias, gamma, beta, out):
    f32, i32 = mybir.dt.float32, mybir.dt.int32
    ALU, ACT, AX = mybir.AluOpType, mybir.ActivationFunctionType, mybir.AxisListType.X

    P = 128
    NODES, D = x.shape
    EDGES, DE = edge_attr.shape
    GC = 14
    GROUPS = 28
    COLS = GC * GROUPS
    FULLP = EDGES // COLS
    REST = EDGES - FULLP * COLS
    assert FULLP == P - 1 and 0 < REST <= COLS
    J = 28
    BLOCKS = GROUPS
    LASTN = NODES - (BLOCKS - 1) * P * J
    LJ = 32
    LP = LASTN // LJ
    assert LP * LJ == LASTN and LP <= P
    JM = max(J, LJ)
    H = GC // 2
    E1 = D + 1
    EPS, SLOPE = 1e-5, 0.01
    BIG = 1e30
    FAR = 1 << 20

    CH = 2000
    CHUNKS = EDGES // CH
    assert CHUNKS * CH == EDGES
    WORDS = 2 + DE

    ranked = nc.dram_tensor("ranked_edges", (EDGES, WORDS), i32).ap()
    spill = nc.dram_tensor("xdst_rows", (P, COLS * D), f32).ap()

    def dense(t, b, last):
        if last:
            return t[(BLOCKS - 1) * P * J:NODES, :].rearrange("(p j) f -> p j f", p=LP)
        return t[bass.ds(b * (P * J), P * J), :].rearrange("(p j) f -> p j f", p=P)

    def group(t, g, n=GC):
        return t[:, bass.ds(g * n, n)]

    ctx = ExitStack()
    with ctx:
        def sb(name, shape, dt=f32):
            return ctx.enter_context(nc.sbuf_tensor(name, shape, dt))

        def sem(name):
            return ctx.enter_context(nc.semaphore(name))

        def pair(name):
            return [sem(f"{name}{b}") for b in range(2)]

        ident = sb("ident", [P, P])
        ones = sb("ones", [P, P])
        eps = sb("eps", [P, 1])
        reach = sb("reach", [P, P])
        far = sb("far", [P, P])
        w1 = sb("w1", [D, D + DE])
        w2 = sb("w2", [D, 2 * D])
        w1d = sb("w1d", [D, 2 * D])
        centre = sb("centre", [D, D])
        al = sb("al", [D, 1])
        alrep = sb("alrep", [D, P])
        rows = sb("rows", [P, 4, D])
        arow, brow, grow, erow = (rows[:, k, :] for k in range(4))
        vrow = sb("vrow", [P, D + DE])
        wc = sb("wc", [P, E1])
        brep = sb("brep", [P, H, E1])
        crow = sb("crow", [P, D])
        sc = sb("sc", [P, 8])
        srci = sb("srci", [P, COLS], i32)
        dsti = sb("dsti", [P, COLS], i32)
        dstg = sb("dstg", [P, COLS], i32)
        nxti = sb("nxti", [P, 1], i32)
        dstf = sb("dstf", [P, COLS])
        nxtf = sb("nxtf", [P, 1])
        ea = sb("ea", [P, COLS])
        fac = sb("fac", [P, 2, COLS])
        fmax = sb("fmax", [P, COLS + 1])
        s1 = sb("s1", [P, COLS])
        pen = sb("pen", [P, COLS + 1])
        same = sb("same", [P, COLS + 1])
        isfirst = sb("isfirst", [P, COLS])
        scat = sb("scat", [P, COLS], i32)
        xt = sb("xt", [P, GROUPS, E1, GC])
        idx = [sb(f"idx{b}", [P, 2, GC], i32) for b in range(2)]
        xs = [sb(f"xs{b}", [P, GC, D]) for b in range(2)]
        xd = [sb(f"xd{b}", [P, GC, D]) for b in range(2)]
        xsT = [sb(f"xsT{b}", [P, H, P]) for b in range(2)]
        xin = [sb(f"xin{b}", [P, JM, D]) for b in range(2)]
        yb = [sb(f"yb{b}", [P, JM, D]) for b in range(2)]
        flag = sb("flag", [P, 2])
        flagi = sb("flagi", [P, 1], i32)
        rec = sb("rec", [P, GC, WORDS], i32)
        reci = sb("reci", [P, GC], i32)
        work = sb("work", [P, GC, D])
        sq = sb("sq", [P, JM, D])
        sq2 = sb("sq2", [P, 2 * GC, D])
        st = sb("st", [P, 4, JM])
        st2 = [sb(f"st2{b}", [P, 4, GC]) for b in range(2)]
        score = sb("score", [P, GC])
        shift = sb("shift", [P, GC])
        down = [sb(f"down{b}", [P, 2, GC]) for b in range(2)]
        decay = sb("decay", [P, E1, GC])
        prev = sb("prev", [P, E1])
        ends = sb("ends", [P, 2, P])
        brought = sb("brought", [P, 1])
        pull = ends[:, 0, :]
        carry = sb("carry", [P, E1])

        psT = [ctx.enter_context(nc.psum_tensor(f"psT{b}", [P, 2, 512], f32)) for b in range(2)]
        psX = [ctx.enter_context(nc.psum_tensor(f"psX{b}", [P, 2, 512], f32)) for b in range(2)]

        s_const = sem("s_const")
        s_ones = sem("s_ones")
        s_pads = sem("s_pads")
        s_load = sem("s_load")
        s_bad = sem("s_bad")
        s_badp = sem("s_badp")
        s_flag = sem("s_flag")
        s_iota = sem("s_iota")
        s_row = sem("s_row")
        s_rowu = sem("s_rowu")
        s_rank = sem("s_rank")
        s_rec = sem("s_rec")
        s_rsc = sem("s_rsc")
        s_again = sem("s_again")
        s_edge = sem("s_edge")
        s_attr = sem("s_attr")
        s_alrep = sem("s_alrep")
        s_wps = sem("s_wps")
        s_wsb = sem("s_wsb")
        s_idx = pair("s_idx")
        s_gs = pair("s_gs")
        s_gd = pair("s_gd")
        s_tr = pair("s_tr")
        s_tc = pair("s_tc")
        s_xm = pair("s_xm")
        s_xc = pair("s_xc")
        s_er = pair("s_er")
        s_sp = pair("s_sp")
        s_xin = pair("s_xin")
        s_xu = pair("s_xu")
        s_yc = pair("s_yc")
        s_sq = pair("s_sq")
        s_y = pair("s_y")
        s_st = pair("s_st")
        s_var = pair("s_var")
        s_dev = pair("s_dev")
        s_bv = sem("s_bv")
        s_bd = sem("s_bd")
        s_v = sem("s_v")
        s_dn = pair("s_dn")
        s_w = pair("s_w")
        s_dc = pair("s_dc")
        s_ends = sem("s_ends")
        s_endp = sem("s_endp")
        s_farr = sem("s_farr")
        s_dia = sem("s_dia")
        s_spr = sem("s_spr")
        s_pl = sem("s_pl")
        s_ple = sem("s_ple")
        s_rch = sem("s_rch")
        s_cps = sem("s_cps")
        s_fc = sem("s_fc")
        s_fe = sem("s_fe")
        s_re = pair("s_re")
        s_a = pair("s_a")
        s_asq = pair("s_asq")
        s_b = pair("s_b")
        s_bsq = pair("s_bsq")
        s_av = pair("s_av")
        s_ad = pair("s_ad")
        s_bvar = pair("s_bvar")
        s_bdev = pair("s_bdev")
        s_bi = pair("s_bi")
        s_z = [sem(f"s_z{q}") for q in range(4)]
        s_sc = [sem(f"s_sc{q}") for q in range(4)]

        attr = xt[:, :, :, :].rearrange("p g f c -> p (g f c)")[:, 0:COLS * DE].rearrange("p (c f) -> p c f", f=DE)

        STEPS_OF_ROUND = 56

        rooms = xt[:, :, :, :].rearrange("p g f c -> p (g f c)")[:, COLS * DE:COLS * DE + 5 * CH].rearrange(
            "p (k n) -> p k n", n=CH)
        rowi, place_i = rooms[:, 0, :].bitcast(i32), rooms[:, 3, :].bitcast(i32)
        rowf, place, less, tie = (rooms[:, k, :] for k in range(1, 5))

        def unsorted(eng):
            eng.wait_ge(s_flag, 1)
            return eng.If(eng.value_load(flagi[0:1, 0:1]) > 0)

        block = ctx.enter_context(nc.Block())

        class Steps:
            base, n = 0, 0

            def __call__(self, ins):
                ins.then_inc(s_v, 1)
                self.n += 1
                nc.vector.wait_ge(s_v, self.base + self.n)

        def rows_of(q):
            return yb[q % 2][:, (q // 2) * GC:(q // 2 + 1) * GC, :]

        def numbers_of(q):
            return idx[q % 2][:, q // 2, :]

        def square_a(b):
            return sq[:, b * GC:(b + 1) * GC, :]

        def square_b(b):
            return sq2[:, b * GC:(b + 1) * GC, :]

        def in_turn(eng, before, work_, after, step=None):
            def round_of_four(r, first=False, last=False):
                for q in range(4):
                    if first and q == 0:
                        work_(0, 0)
                        after(0, 0)
                        before(1, 0)
                        continue
                    if not (last and q == 3):
                        before((q + 1) % 4, r + (q + 1) // 4)
                    work_(q, r)
                    if not (first and q == 1):
                        after((q - 1) % 4, r + (q - 1) // 4)

            rounds = GROUPS // 4
            before(0, 0)
            round_of_four(0, first=True)
            if step:
                start, step.n = step.n, 0
            with eng.Fori(1, rounds - 1) as r:
                if step:
                    step.base = (r - 1) * STEPS_OF_ROUND + start
                round_of_four(r)
            if step:
                assert step.n == STEPS_OF_ROUND, step.n
                step.base, step.n = 0, start + (rounds - 2) * STEPS_OF_ROUND
            round_of_four(rounds - 1, last=True)
            after(3, rounds - 1)

        def wait_free(eng, s, count):
            if not (isinstance(count, int) and count == 0):
                eng.wait_ge(s, count)

        def sums_of(b):
            return xin[b][:, 0:GC, :]

        def over(row, n, width=D):
            return row.unsqueeze(1).broadcast_to([row.shape[0], n, width])

        def along(cols, width=D):
            return cols.unsqueeze(2).broadcast_to([cols.shape[0], cols.shape[1], width])

        @block.sync
        def _(sp):
            def edges(to, a, s):
                with nc.allow_non_contiguous_dma(reason="sorted edges are loaded word by word"):
                    sp.dma_start(to[0:FULLP], a[0:FULLP * COLS].rearrange("(p c) ... -> p c ...", p=FULLP)
                                 ).then_inc(s, 16)
                    sp.dma_start(to[FULLP:P, 0:REST], a[FULLP * COLS:EDGES].rearrange("(p c) ... -> p c ...", p=1)
                                 ).then_inc(s, 16)

            def neighbours(a, s):
                with nc.allow_non_contiguous_dma(reason="one number for each partition"):
                    sp.dma_start(nxti[0:FULLP, :], a[COLS:EDGES:COLS, :]).then_inc(s, 16)

            sp.wait_ge(s_pads, 1)
            edges(dsti[:, :], dst, s_edge)
            neighbours(dst.unsqueeze(1), s_edge)
            edges(srci[:, :], src, s_edge)
            for b in range(2):
                sp.dma_start(xin[b][:, 0:J, :], dense(x, b, False)).then_inc(s_xin[b], 16)
            sp.dma_start(w1[:, :], W1).then_inc(s_load, 16)
            for k in range(2):
                sp.dma_start(w2[:, k * D:(k + 1) * D], W2).then_inc(s_load, 16)
                sp.dma_start(w1d[:, k * D:(k + 1) * D], W1[:, 0:D]).then_inc(s_load, 16)
            with nc.allow_non_contiguous_dma(reason="one number for each partition"):
                sp.dma_start(al[:, :], att_l.unsqueeze(1)).then_inc(s_load, 16)
            for k, row in enumerate((att_r, bias, gamma, beta)):
                sp.dma_start(rows[:, k, :], row.unsqueeze(0).broadcast_to([P, D])).then_inc(s_load, 16)
            sp.wait_ge(s_pads, 2)
            edges(attr, edge_attr, s_attr)

            with unsorted(sp):
                def chunk(k):
                    sp.dma_start(rowi, dst[bass.ds(k * CH, CH)].unsqueeze(0).broadcast_to([P, CH])).then_inc(s_row, 16)

                chunk(0)
                with sp.Fori(1, CHUNKS) as k:
                    sp.wait_ge(s_rowu, k)
                    chunk(k)
                sp.wait_ge(s_rsc, 16 * COLS)
                edges(dsti[:, :], ranked[:, 1], s_again)
                neighbours(ranked[:, 1:2], s_again)
                edges(srci[:, :], ranked[:, 0], s_again)
                edges(attr.bitcast(i32), ranked[:, 2:WORDS], s_again)

            def stores(i, last):
                for b in range(2):
                    g = i * 2 + b
                    end = last and b == 1
                    np_, nj = (LP, LJ) if end else (P, J)
                    if not last:
                        sp.wait_ge(s_xu[b], i + 1)
                        sp.dma_start(xin[b][:, 0:J, :], dense(x, g + 2, False)).then_inc(s_xin[b], 16)
                    sp.wait_ge(s_y[b], i + 1)
                    sp.dma_start(dense(out, g, end), yb[b][0:np_, 0:nj, :]).then_inc(s_st[b], 16)
                    sp.wait_ge(s_er[b], i + 1)
                    sp.dma_start(group(spill, g, GC * D), xd[b][:, :, :].rearrange("p c f -> p (c f)")
                                 ).then_inc(s_sp[b], 16)

            pairs = GROUPS // 2
            with sp.Fori(0, pairs - 2) as i:
                stores(i, False)
            i = pairs - 2
            for b in range(2):
                sp.wait_ge(s_xu[b], i + 1)
                np_, nj = (LP, LJ) if b else (P, J)
                sp.dma_start(xin[b][0:np_, 0:nj, :], dense(x, 2 * i + b + 2, b == 1)).then_inc(s_xin[b], 16)
                sp.wait_ge(s_y[b], i + 1)
                sp.dma_start(dense(out, 2 * i + b, False), yb[b][:, 0:J, :]).then_inc(s_st[b], 16)
                sp.wait_ge(s_er[b], i + 1)
                sp.dma_start(group(spill, 2 * i + b, GC * D), xd[b][:, :, :].rearrange("p c f -> p (c f)")
                             ).then_inc(s_sp[b], 16)
            stores(pairs - 1, True)

            for b in range(2):
                sp.wait_ge(s_sp[b], 16 * pairs)
            for b in range(2):
                sp.dma_start(xd[b][:, :, :].rearrange("p c f -> p (c f)"), group(spill, b, GC * D)
                             ).then_inc(s_re[b], 16)
            with sp.Fori(0, pairs - 1) as i:
                for b in range(2):
                    sp.wait_ge(s_b[b], i + 1)
                    sp.dma_start(xd[b][:, :, :].rearrange("p c f -> p (c f)"), group(spill, i * 2 + b + 2, GC * D)
                                 ).then_inc(s_re[b], 16)
            for b in range(2):
                sp.wait_ge(s_st[b], 16 * pairs)

        @block.gpsimd
        def _(pool):
            nc.gpsimd.memset(dsti[:, :], FAR)
            nc.gpsimd.memset(nxti[:, :], 2 * FAR)
            nc.gpsimd.memset(srci[:, :], 0).then_inc(s_pads, 1)
            nc.gpsimd.memset(ones[:, :], 1.0).then_inc(s_ones, 1)
            nc.gpsimd.memset(attr, 0.0).then_inc(s_pads, 1)
            nc.gpsimd.memset(ident[:, :], 0.0)
            nc.gpsimd.memset(eps[:, :], EPS)
            nc.gpsimd.memset(centre[:, :], -1.0 / D).then_inc(s_const, 1)
            pool.wait_ge(s_const, 1)
            nc.gpsimd.affine_select(out=ident[:, :], in_=ident[:, :], compare_op=ALU.not_equal, fill=1.0,
                                    base=0, pattern=[[1, P]], channel_multiplier=-1)
            nc.gpsimd.affine_select(out=reach[:, :], in_=ones[:, :], compare_op=ALU.is_gt, fill=0.0,
                                    base=0, pattern=[[1, P]], channel_multiplier=-1)
            nc.gpsimd.affine_select(out=far[:, :], in_=ones[:, :], compare_op=ALU.is_gt, fill=0.0,
                                    base=0, pattern=[[-1, P]], channel_multiplier=1)
            nc.gpsimd.affine_select(out=centre[:, :], in_=centre[:, :], compare_op=ALU.not_equal, fill=1.0 - 1.0 / D,
                                    base=0, pattern=[[1, D]], channel_multiplier=-1).then_inc(s_const, 1)

            with unsorted(pool):
                nc.gpsimd.iota(ea[:, :].bitcast(i32), pattern=[[1, COLS]], base=0, channel_multiplier=COLS)
                nc.gpsimd.iota(place_i, pattern=[[1, CH]], base=0, channel_multiplier=0).then_inc(s_iota, 1)
                pool.wait_ge(s_attr, 32)
                pool.wait_ge(s_rank, 1)
                with pool.Fori(0, GROUPS) as g:
                    now, out_ = pool.to_reg(g + 1), pool.to_reg(g * (16 * GC) + 16 * GC)
                    nc.gpsimd.tensor_copy(rec[:, :, 0], group(srci, g))
                    nc.gpsimd.tensor_copy(rec[:, :, 1], group(dsti, g))
                    nc.gpsimd.tensor_copy(rec[:, :, 2:WORDS], attr[:, bass.ds(g * GC, GC), :].bitcast(i32))
                    nc.gpsimd.tensor_copy(reci[:, :], group(scat, g)).then_inc(s_rec, 1)
                    pool.wait_ge(s_const, 1)
                    pool.wait_ge(s_rec, now)
                    for k in range(GC):
                        nc.gpsimd.indirect_dma_start(ranked[:, :], bass.IndirectOffsetOnAxis(
                            ap=reci[:, k:k + 1], axis=0), rec[:, k, :], None,
                            bounds_check=EDGES - 1, oob_is_err=False).then_inc(s_rsc, 16)
                    pool.wait_ge(s_const, 1)
                    pool.wait_ge(s_rsc, out_)

            def gathers(i):
                first = isinstance(i, int)
                before, after, spilled = (i, i + 1, i * 16) if first else (
                    i, pool.to_reg(i + 1), pool.to_reg(i * 16))
                for b in range(2):
                    pool.wait_ge(s_const, 1)
                    pool.wait_ge(s_idx[b], after)
                    wait_free(pool, s_tr[b], before)
                    for k in range(GC):
                        nc.gpsimd.indirect_dma_start(xs[b][:, k, :], None, x[:, :], bass.IndirectOffsetOnAxis(
                            ap=idx[b][:, 0, k:k + 1], axis=0)).then_inc(s_gs[b], 16)
                    pool.wait_ge(s_const, 1)
                    wait_free(pool, s_sp[b], spilled)
                    for k in range(GC):
                        nc.gpsimd.indirect_dma_start(xd[b][:, k, :], None, x[:, :], bass.IndirectOffsetOnAxis(
                            ap=idx[b][:, 1, k:k + 1], axis=0)).then_inc(s_gd[b], 16)

            gathers(0)
            with pool.Fori(1, GROUPS // 2) as i:
                gathers(i)

            for b in range(2):
                pool.wait_ge(s_st[b], 16 * (GROUPS // 2))
            with pool.Fori(0, GROUPS // 4) as r:
                after = pool.to_reg(r + 1)
                for q in range(4):
                    pool.wait_ge(s_const, 1)
                    pool.wait_ge(s_z[q], after)
                    for k in range(GC):
                        nc.gpsimd.indirect_dma_start(out[:, :], bass.IndirectOffsetOnAxis(
                            ap=numbers_of(q)[:, k:k + 1], axis=0), rows_of(q)[:, k, :], None,
                            bounds_check=NODES - 1, oob_is_err=False).then_inc(s_sc[q], 16)
            for q in range(4):
                pool.wait_ge(s_sc[q], 16 * GC * (GROUPS // 4))

        @block.scalar
        def _(act):
            def deviation(total):
                return nc.scalar.activation(total, total, ACT.Sqrt, scale=1.0 / D, bias=eps[0:total.shape[0], :])

            act.wait_ge(s_const, 1)
            act.wait_ge(s_bv, 1)
            deviation(sc[:, 1:2]).then_inc(s_bd, 1)

            def part(i, last):
                for b in range(2):
                    np_, nj = (LP, LJ) if last and b == 1 else (P, J)
                    act.wait_ge(s_tr[b], i + 1)
                    wait_free(act, s_xm[b], i)
                    nc.scalar.copy(xsT[b][:, 0:4, :].rearrange("p k e -> p (k e)"), psT[b][:, 0, :])
                    nc.scalar.copy(xsT[b][:, 4:H, :].rearrange("p k e -> p (k e)"), psT[b][:, 1, 0:(H - 4) * P]
                                   ).then_inc(s_tc[b], 1)
                    act.wait_ge(s_yc[b], i + 1)
                    nc.scalar.activation(sq[0:np_, 0:nj, :], yb[b][0:np_, 0:nj, :], ACT.Square).then_inc(s_sq[b], 1)
                    act.wait_ge(s_var[b], i + 1)
                    deviation(st[0:np_, 1, 0:nj]).then_inc(s_dev[b], 1)
                    act.wait_ge(s_dn[b], i + 1)
                    nc.scalar.activation(down[b][:, :, :], down[b][:, :, :], ACT.Exp).then_inc(s_w[b], 1)
                    act.wait_ge(s_w[b], i + 1)
                    nc.scalar.copy(decay[:, :, 1:GC], over(down[b][:, 0, 1:GC], E1, GC - 1)).then_inc(s_dc[b], 1)

            part(0, False)
            with act.Fori(1, GROUPS // 2 - 1) as i:
                part(i, False)
            part(GROUPS // 2 - 1, True)
            act.wait_ge(s_pl, 1)
            nc.scalar.activation(pull, pull, ACT.Exp).then_inc(s_ple, 1)
            act.wait_ge(s_fc, 1)
            nc.scalar.activation(fac[:, :, :], fac[:, :, :], ACT.Exp).then_inc(s_fe, 1)

            def squares_of_sums(q, r):
                b, i = q % 2, r * 2 + q // 2
                act.wait_ge(s_a[b], i + 1)
                nc.scalar.activation(square_a(b), sums_of(b), ACT.Square).then_inc(s_asq[b], 1)

            def middle(q, r):
                b, i = q % 2, r * 2 + q // 2
                act.wait_ge(s_av[b], i + 1)
                deviation(st2[b][:, 1, :]).then_inc(s_ad[b], 1)
                act.wait_ge(s_b[b], i + 1)
                nc.scalar.activation(square_b(b), rows_of(q), ACT.Square).then_inc(s_bsq[b], 1)

            def scaled(q, r):
                b, i = q % 2, r * 2 + q // 2
                act.wait_ge(s_bvar[b], i + 1)
                deviation(st2[b][:, 3, :]).then_inc(s_bdev[b], 1)
                act.wait_ge(s_bi[b], i + 1)
                for k in range(GC):
                    last_row = nc.scalar.mul(rows_of(q)[:, k, :], rows_of(q)[:, k, :], st2[b][:, 3, k:k + 1])
                last_row.then_inc(s_z[q], 1)

            in_turn(act, squares_of_sums, middle, scaled)

        @block.tensor
        def _(pe):
            pe.wait_ge(s_ones, 1)
            pe.wait_ge(s_bad, 1)
            nc.tensor.matmul(psT[1][:, 1, 0:1], ones[:, :], flag[:, 0:1], start=True, stop=True).then_inc(s_badp, 1)
            pe.wait_ge(s_load, 16 * 10)
            pe.wait_ge(s_alrep, 1)
            nc.tensor.matmul(psT[0][:, 0, 0:D + DE], alrep[:, :], w1[:, :], start=True, stop=True)
            nc.tensor.matmul(psT[0][:, 1, 0:D], w2[:, :], centre[:, :], start=True, stop=True)
            nc.tensor.matmul(psT[1][:, 0, 0:1], w1d[:, :], al[:, :], start=True, stop=True).then_inc(s_wps, 1)
            pe.wait_ge(s_wsb, 1)
            pe.wait_ge(s_ends, 1)
            nc.tensor.matmul(psX[0][:, 0, 0:2 * P], ones[:, :], ends[:, :, :].rearrange("p k q -> p (k q)"),
                             start=True, stop=True).then_inc(s_endp, 1)
            pe.wait_ge(s_farr, 1)

            def products(i):
                for b in range(2):
                    pe.wait_ge(s_gs[b], i * (16 * GC) + 16 * GC)
                    wait_free(pe, s_tc[b], i)
                    for k in range(H):
                        last = nc.tensor.transpose(psT[b][:, k // 4, (k % 4) * P:(k % 4 + 1) * P],
                                                   xs[b][:, 2 * k:2 * k + 2, :].rearrange("p c f -> p (c f)"),
                                                   ident[:, :])
                    last.then_inc(s_tr[b], 1)
                    pe.wait_ge(s_tc[b], i + 1)
                    wait_free(pe, s_xc[b], i)
                    for h in range(2):
                        half = slice(D * h, D * (h + 1))
                        nc.tensor.matmul(psX[b][:, h, 0:H * E1], ones[half, :],
                                         brep[half, :, :].rearrange("p c f -> p (c f)"), start=True, stop=False)
                        for k in range(H):
                            last = nc.tensor.matmul(psX[b][:, h, k * E1:(k + 1) * E1], xsT[b][half, k, :],
                                                    wc[half, :], start=False, stop=(k == H - 1))
                    last.then_inc(s_xm[b], 1)

            products(0)
            with pe.Fori(1, GROUPS // 2) as i:
                products(i)
            for b in range(2):
                pe.wait_ge(s_tc[b], GROUPS // 2)
            for k in range(2):
                pe.wait_ge(s_dia, k + 1)
                nc.tensor.matmul(psT[k][:, 0, 0:P], ones[:, :], ends[:, k, :], start=True, stop=True).then_inc(s_spr, 1)
            pe.wait_ge(s_xc[0], GROUPS // 2)
            pe.wait_ge(s_rch, 1)
            nc.tensor.matmul(psX[0][:, 0, 0:E1], pull, prev[:, :], start=True, stop=True).then_inc(s_cps, 1)

        @block.vector
        def _(dve):
            V = nc.vector
            step = Steps()

            def done(ins, s, count):
                ins.then_inc(s, 1)
                dve.wait_ge(s, count)

            def copy_idx(g, b):
                V.tensor_copy(idx[b][:, 0, :], group(srci, g))
                V.tensor_copy(idx[b][:, 1, :], group(dstg, g)).then_inc(s_idx[b], 1)

            dfirst, dlast = dstf[:, 0:1], dstf[:, COLS - 1:COLS]
            dve.wait_ge(s_edge, 16 * 5)
            V.tensor_copy(nxtf[:, :], nxti[:, :])
            step(V.tensor_copy(dstf[:, :], dsti[:, :]))
            V.tensor_tensor(same[:, 0:COLS - 1], dstf[:, 1:COLS], dstf[:, 0:COLS - 1], ALU.is_lt)
            step(V.tensor_tensor(same[:, COLS - 1:COLS], nxtf[:, :], dlast, ALU.is_lt))
            V.tensor_reduce(flag[:, 0:1], same[:, 0:COLS], AX, ALU.add).then_inc(s_bad, 1)
            dve.wait_ge(s_badp, 1)
            V.tensor_copy(flagi[:, :], psT[1][:, 1, 0:1]).then_inc(s_flag, 1)

            with unsorted(dve):
                def then(ins):
                    dve.drain()

                rank = fac[:, 0, :]
                dve.wait_ge(s_iota, 1)
                V.tensor_copy(place, place_i)
                then(V.tensor_copy(s1[:, :], ea[:, :].bitcast(i32)))
                then(V.memset(rank, 0.0))
                with dve.Fori(0, CHUNKS) as k:
                    dve.wait_ge(s_row, k * 16 + 16)
                    V.tensor_copy(rowf, rowi).then_inc(s_rowu, 1)
                    dve.drain()
                    with dve.Fori(0, COLS) as c:
                        mine = dstf[:, bass.ds(c, 1)]
                        V.tensor_scalar(less, rowf, mine, None, ALU.is_lt)
                        then(V.tensor_scalar(tie, place, s1[:, bass.ds(c, 1)], None, ALU.is_lt))
                        then(V.scalar_tensor_tensor(tie, rowf, mine, tie, ALU.is_equal, ALU.mult))
                        then(V.tensor_tensor(less, less, tie, ALU.add))
                        then(V.tensor_reduce(flag[:, 1:2], less, AX, ALU.add))
                        then(V.tensor_tensor(rank[:, bass.ds(c, 1)], rank[:, bass.ds(c, 1)], flag[:, 1:2], ALU.add))
                    then(V.tensor_scalar(s1[:, :], s1[:, :], float(CH), None, ALU.subtract))
                V.tensor_copy(scat[:, :], rank).then_inc(s_rank, 1)
                dve.wait_ge(s_again, 16 * 7)
                V.tensor_copy(nxtf[:, :], nxti[:, :])
                then(V.tensor_copy(dstf[:, :], dsti[:, :]))

            step(V.scalar_tensor_tensor(dstg[:, :], dstf[:, :], float(FAR), dstf[:, :], ALU.is_lt, ALU.mult))
            for b in range(2):
                copy_idx(b, b)
            dve.wait_ge(s_load, 16 * 10)
            dve.wait_ge(s_const, 2)
            V.tensor_copy(alrep[:, :], al[:, 0:1].broadcast_to([D, P])).then_inc(s_alrep, 1)
            step(V.tensor_reduce(sc[:, 0:1], brow, AX, ALU.add))
            step(V.tensor_scalar(sc[:, 0:1], sc[:, 0:1], 1.0 / D, None, ALU.mult))
            step(V.tensor_scalar(brow, brow, sc[:, 0:1], None, ALU.subtract))
            step(V.tensor_tensor(crow[:, :], brow, brow, ALU.mult))
            V.tensor_reduce(sc[:, 1:2], crow[:, :], AX, ALU.add).then_inc(s_bv, 1)
            dve.wait_ge(s_bd, 1)
            step(V.reciprocal(sc[:, 2:3], sc[:, 1:2]))
            step(V.tensor_scalar(crow[:, :], brow, sc[:, 2:3], None, ALU.mult))
            step(V.tensor_tensor(crow[:, :], crow[:, :], grow, ALU.mult))
            step(V.tensor_tensor(crow[:, :], crow[:, :], erow, ALU.add))
            step(V.memset(brep[:, :, :], 0.0))
            step(V.tensor_scalar(brep[:, :, 0:D], over(brow, H), 1.0 / D, None, ALU.mult))
            dve.wait_ge(s_wps, 1)
            step(V.tensor_copy(vrow[:, :], psT[0][:, 0, 0:D + DE]))
            step(V.tensor_copy(wc[:, 0:D], psT[0][:, 1, 0:D]))
            done(V.tensor_copy(wc[:, D:E1], psT[1][:, 0, 0:1]), s_wsb, 1)
            dve.wait_ge(s_attr, 32)
            step(V.tensor_tensor(attr, attr, over(vrow[:, D:D + DE], COLS, DE), ALU.mult))
            step(V.tensor_reduce(ea[:, :], attr, AX, ALU.add))

            step(V.memset(same[:, 0:1], 0.0))
            V.tensor_tensor(same[:, 1:COLS], dstf[:, 1:COLS], dstf[:, 0:COLS - 1], ALU.is_equal)
            step(V.tensor_tensor(same[:, COLS:COLS + 1], dlast, nxtf[:, :], ALU.is_equal))
            V.tensor_scalar(pen[:, :], same[:, :], 1.0, BIG, ALU.subtract, ALU.mult)
            V.tensor_scalar(isfirst[:, :], dstf[:, :], dfirst, None, ALU.is_equal)
            V.memset(decay[:, :, 0:1], 0.0)
            V.memset(prev[:, :], 0.0)
            V.memset(fmax[:, 0:1], -BIG)
            step(V.scalar_tensor_tensor(s1[:, :], same[:, 1:COLS + 1], float(FAR), dstf[:, :], ALU.mult, ALU.add))
            V.tensor_copy(scat[:, :], s1[:, :])
            for k, end in enumerate((dfirst, dlast)):
                ins = V.tensor_scalar(ends[:, k, :], ident[:, :], end, None, ALU.mult)
            ins.then_inc(s_ends, 1)
            dve.wait_ge(s_endp, 1)
            spread = psX[0][:, 0, 0:2 * P].rearrange("p (k q) -> p k q", q=P)
            step(V.scalar_tensor_tensor(reach[:, :], spread[:, 0, :], dlast, reach[:, :], ALU.is_equal, ALU.mult))
            step(V.scalar_tensor_tensor(far[:, :], spread[:, 1, :], dfirst, far[:, :], ALU.is_equal, ALU.mult))
            done(V.tensor_scalar(far[:, :], far[:, :], 1.0, BIG, ALU.subtract, ALU.mult), s_farr, 1)

            def part(i, last):
                for b in range(2):
                    g = i * 2 + b
                    np_, nj = (LP, LJ) if last and b == 1 else (P, J)
                    y, q, t = yb[b][0:np_, 0:nj, :], sq[0:np_, 0:nj, :], st[0:np_, :, 0:nj]
                    dve.wait_ge(s_xin[b], i * 16 + 16)
                    wait_free(dve, s_st[b], i * 16)
                    done(V.tensor_tensor(y, xin[b][0:np_, 0:nj, :], over(crow[0:np_, :], nj), ALU.add), s_xu[b], i + 1)
                    step(V.tensor_reduce(t[:, 0, :], y, AX, ALU.add))
                    step(V.tensor_scalar(t[:, 0, :], t[:, 0, :], 1.0 / D, None, ALU.mult))
                    done(V.tensor_tensor(y, y, along(t[:, 0, :]), ALU.subtract), s_yc[b], i + 1)
                    dve.wait_ge(s_sq[b], i + 1)
                    V.tensor_reduce(t[:, 1, :], q, AX, ALU.add).then_inc(s_var[b], 1)
                    dve.wait_ge(s_dev[b], i + 1)
                    step(V.reciprocal(t[:, 1, :], t[:, 1, :]))
                    V.tensor_tensor(y, y, along(t[:, 1, :]), ALU.mult).then_inc(s_y[b], 1)
                    dve.wait_ge(s_gs[b], i * (16 * GC) + 16 * GC)
                    dve.wait_ge(s_gd[b], i * (16 * GC) + 16 * GC)
                    if not last:
                        copy_idx(g + 2, b)
                    step(V.tensor_tensor(work[:, :, :], xd[b][:, :, :], over(arow, GC), ALU.mult))
                    step(V.tensor_reduce(score[:, :], work[:, :, :], AX, ALU.add))
                    V.tensor_tensor(xd[b][:, :, :], xd[b][:, :, :], over(erow, GC), ALU.add).then_inc(s_er[b], 1)
                    step(V.tensor_tensor(score[:, :], score[:, :], group(ea, g), ALU.add))
                    dve.wait_ge(s_xm[b], i + 1)
                    product = psX[b][:, :, 0:H * E1].rearrange("p h (k f) -> p h k f", f=E1)
                    by_bank = "p (k h) -> p h k"
                    halves = score[:, :].rearrange(by_bank, h=2)
                    step(V.tensor_tensor(halves, halves, product[:, :, :, D], ALU.add))
                    step(V.scalar_tensor_tensor(score[:, :], score[:, :], SLOPE, score[:, :], ALU.mult, ALU.max))
                    before, now = group(fmax, g), fmax[:, bass.ds(g * GC + 1, GC)]
                    step(V.tensor_tensor_scan(now, group(pen, g), score[:, :], before[:, 0:1], ALU.add, ALU.max))
                    V.tensor_tensor(down[b][:, 1, :], score[:, :], now, ALU.subtract)
                    step(V.tensor_tensor(shift[:, :], before, group(pen, g), ALU.add))
                    V.tensor_tensor(down[b][:, 0, :], shift[:, :], now, ALU.subtract).then_inc(s_dn[b], 1)
                    dve.wait_ge(s_w[b], i + 1)
                    rows_ = xt[:, bass.ds(g, 1), :, :].rearrange("p g f c -> p (g f) c")
                    V.tensor_copy(rows_[:, D, :], down[b][:, 1, :])
                    into = rows_[:, 0:D, :].rearrange("p f (k h) -> p h k f", h=2)
                    weight = down[b][:, 1, :].rearrange(by_bank, h=2)
                    for h in range(2):
                        ins = V.tensor_tensor(into[:, h], product[:, h, :, 0:D], along(weight[:, h, :]), ALU.mult)
                    done(ins, s_xc[b], i + 1)
                    step(V.scalar_tensor_tensor(rows_[:, :, 0], prev[:, :], down[b][:, 0, 0:1], rows_[:, :, 0],
                                                ALU.mult, ALU.add))
                    dve.wait_ge(s_dc[b], i + 1)
                    flat = rows_.rearrange("p f c -> p (f c)")
                    step(V.tensor_tensor_scan(flat, decay[:, :, :].rearrange("p f c -> p (f c)"), flat, 0.0,
                                              ALU.mult, ALU.add))
                    step(V.tensor_copy(prev[:, :], rows_[:, :, GC - 1]))

            def repeat(count, body):
                start = step.n
                body(0)
                assert step.n == start + PER[body.__name__], (body.__name__, step.n - start)
                with dve.Fori(1, count) as i:
                    step.base, step.n = i * PER[body.__name__] + start, 0
                    body(i)
                step.base, step.n = 0, start + count * PER[body.__name__]

            PER = {"dense_and_er": 2 * 13}

            def dense_and_er(i):
                part(i, False)

            repeat(GROUPS // 2 - 1, dense_and_er)
            part(GROUPS // 2 - 1, True)

            for k, end in enumerate((fmax[:, COLS:COLS + 1], brought[:, :])):
                if k == 1:
                    step(V.tensor_tensor(far[:, :], psT[0][:, 0, 0:P], far[:, :], ALU.add))
                    step(V.tensor_reduce(brought[:, :], far[:, :], AX, ALU.max))
                V.tensor_scalar(ends[:, k, :], ident[:, :], end, None, ALU.mult).then_inc(s_dia, 1)
                dve.wait_ge(s_spr, k + 1)
            step(V.tensor_scalar(pull, psT[1][:, 0, 0:P], -1.0, fmax[:, COLS:COLS + 1], ALU.mult, ALU.add))
            V.tensor_scalar(pull, pull, 0.0, None, ALU.min).then_inc(s_pl, 1)
            top = s1[:, :]
            step(V.tensor_scalar(top, fmax[:, 1:COLS + 1], brought[:, :], None, ALU.max))
            V.tensor_scalar(fac[:, 1, :], top, -1.0, brought[:, :], ALU.mult, ALU.add)
            step(V.tensor_tensor(fac[:, 0, :], fmax[:, 1:COLS + 1], top, ALU.subtract))
            V.tensor_tensor(fac[:, 0, :], fac[:, 0, :], isfirst[:, :], ALU.mult).then_inc(s_fc, 1)
            dve.wait_ge(s_ple, 1)
            done(V.tensor_tensor(pull, pull, reach[:, :], ALU.mult), s_rch, 1)
            dve.wait_ge(s_fe, 1)
            step(V.tensor_tensor(fac[:, 1, :], fac[:, 1, :], isfirst[:, :], ALU.mult))
            dve.wait_ge(s_cps, 1)
            step(V.tensor_copy(carry[:, :], psX[0][:, 0, 0:E1]))

            for b in range(2):
                dve.wait_ge(s_st[b], 16 * (GROUPS // 2))

            def sums(q, r):
                b, i, g = q % 2, r * 2 + q // 2, r * 4 + q
                own = xt[:, bass.ds(g, 1), :, :].rearrange("p g f c -> p c (g f)")
                V.tensor_tensor(work[:, :, :], along(group(fac[:, 1, :], g)), over(carry[:, 0:D], GC), ALU.mult)
                step(V.tensor_tensor(sums_of(b), own[:, :, 0:D], along(group(fac[:, 0, :], g)), ALU.mult))
                V.tensor_tensor(sums_of(b), sums_of(b), work[:, :, :], ALU.add).then_inc(s_a[b], 1)
                dve.wait_ge(s_a[b], i + 1)

            def rows_out(q, r):
                b, i, g = q % 2, r * 2 + q // 2, r * 4 + q
                y = rows_of(q)
                den, rs, mu, _ = (st2[b][:, k, :] for k in range(4))
                own = xt[:, bass.ds(g, 1), :, :].rearrange("p g f c -> p c (g f)")
                step(V.tensor_tensor(den, own[:, :, D], group(fac[:, 0, :], g), ALU.mult))
                step(V.scalar_tensor_tensor(den, group(fac[:, 1, :], g), carry[:, D:E1], den, ALU.mult, ALU.add))
                step(V.tensor_scalar(den, den, 1e-30, None, ALU.max))
                step(V.reciprocal(den, den))
                dve.wait_ge(s_asq[b], i + 1)
                step(V.tensor_reduce(rs, square_a(b), AX, ALU.add))
                step(V.tensor_tensor(rs, rs, den, ALU.mult))
                V.tensor_tensor(rs, rs, den, ALU.mult).then_inc(s_av[b], 1)
                wait_free(dve, s_sc[q], r * (16 * GC))
                V.tensor_copy(numbers_of(q), group(scat, g))
                dve.wait_ge(s_ad[b], i + 1)
                step(V.reciprocal(rs, rs))
                step(V.tensor_tensor(rs, rs, den, ALU.mult))
                step(V.tensor_tensor(y, sums_of(b), along(rs), ALU.mult))
                step(V.tensor_tensor(y, y, over(grow, GC), ALU.mult))
                dve.wait_ge(s_re[b], i * 16 + 16)
                step(V.tensor_tensor(y, y, xd[b][:, :, :], ALU.add))
                step(V.tensor_reduce(mu, y, AX, ALU.add))
                step(V.tensor_scalar(mu, mu, 1.0 / D, None, ALU.mult))
                V.tensor_tensor(y, y, along(mu), ALU.subtract).then_inc(s_b[b], 1)

            def variances(q, r):
                b, i = q % 2, r * 2 + q // 2
                dv = st2[b][:, 3, :]
                dve.wait_ge(s_bsq[b], i + 1)
                V.tensor_reduce(dv, square_b(b), AX, ALU.add).then_inc(s_bvar[b], 1)
                dve.wait_ge(s_bdev[b], i + 1)
                V.reciprocal(dv, dv).then_inc(s_bi[b], 1)

            in_turn(dve, sums, rows_out, variances, step)


def kernel(**inputs):
    import numpy as _np
    import concourse.bacc as _bacc
    from concourse import mybir as _mybir
    from concourse.bass_utils import run_bass_kernel_spmd as _run

    nc = _bacc.Bacc("TRN2", target_bir_lowering=False, num_devices=1)
    arrays, args = {}, []
    for name in ("x", "src", "dst", "edge_attr_16", "L0_gnn_W1", "L0_gnn_W2", "L0_gnn_att_l", "L0_gnn_att_r",
                 "L0_gnn_bias", "L0_gnn_ln_gamma", "L0_gnn_ln_beta"):
        a = _np.ascontiguousarray(inputs[name])
        arrays[f"in_{name}_dram"] = a
        args.append(nc.dram_tensor(f"in_{name}_dram", a.shape, _mybir.dt.from_np(a.dtype), kind="ExternalInput").ap())
    args.append(nc.dram_tensor("out_0_dram", (100000, 64), _mybir.dt.float32, kind="ExternalOutput").ap())
    gnn_resnorm(nc, *args)
    r = _run(nc, [arrays], core_ids=[0])
    return r.results[0]["out_0_dram"]
```

```python
import concourse.bass as bass
from concourse import mybir
from contextlib import ExitStack


def gnn_resnorm(nc, x, src, dst, edge_attr, W1, W2, att_l, att_r, bias, gamma, beta, out):
    f32, i32 = mybir.dt.float32, mybir.dt.int32
    ALU, ACT, AX = mybir.AluOpType, mybir.ActivationFunctionType, mybir.AxisListType.X

    P = 128
    NODES, D = x.shape
    EDGES, DE = edge_attr.shape
    GC = 14
    GROUPS = 28
    COLS = GC * GROUPS
    FULLP = EDGES // COLS
    REST = EDGES - FULLP * COLS
    assert FULLP == P - 1 and 0 < REST <= COLS
    J = 28
    BLOCKS = GROUPS
    LASTN = NODES - (BLOCKS - 1) * P * J
    LJ = 32
    LP = LASTN // LJ
    assert LP * LJ == LASTN and LP <= P
    JM = max(J, LJ)
    H = GC // 2
    E1 = D + 1
    EPS, SLOPE = 1e-5, 0.01
    BIG = 1e30
    FAR = 1 << 20

    CH = 2000
    CHUNKS = EDGES // CH
    assert CHUNKS * CH == EDGES
    WORDS = 2 + DE

    ranked = nc.dram_tensor("ranked_edges", (EDGES, WORDS), i32).ap()
    spill = nc.dram_tensor("xdst_rows", (P, COLS * D), f32).ap()
    run_sums = nc.dram_tensor("run_sums", (P * GROUPS, (D + 1) * GC), f32).ap()

    def dense(t, b, last):
        if last:
            return t[(BLOCKS - 1) * P * J:NODES, :].rearrange("(p j) f -> p j f", p=LP)
        return t[bass.ds(b * (P * J), P * J), :].rearrange("(p j) f -> p j f", p=P)

    def group(t, g, n=GC):
        return t[:, bass.ds(g * n, n)]

    ctx = ExitStack()
    with ctx:
        def sb(name, shape, dt=f32):
            return ctx.enter_context(nc.sbuf_tensor(name, shape, dt))

        def sem(name):
            return ctx.enter_context(nc.semaphore(name))

        def pair(name):
            return [sem(f"{name}{b}") for b in range(2)]

        ident = sb("ident", [P, P])
        ones = sb("ones", [P, P])
        eps = sb("eps", [P, 1])
        reach = sb("reach", [P, P])
        far = sb("far", [P, P])
        w1 = sb("w1", [D, D + DE])
        w2 = sb("w2", [D, 2 * D])
        w1d = sb("w1d", [D, 2 * D])
        centre = sb("centre", [D, D])
        al = sb("al", [D, 1])
        alrep = sb("alrep", [D, P])
        rows = sb("rows", [P, 4, D])
        arow, brow, grow, erow = (rows[:, k, :] for k in range(4))
        vrow = sb("vrow", [P, D + DE])
        wc = sb("wc", [P, E1])
        brep = sb("brep", [P, H, E1])
        crow = sb("crow", [P, D])
        sc = sb("sc", [P, 8])
        srci = sb("srci", [P, COLS], i32)
        dsti = sb("dsti", [P, COLS], i32)
        dstg = sb("dstg", [P, COLS], i32)
        nxti = sb("nxti", [P, 1], i32)
        dstf = sb("dstf", [P, COLS])
        nxtf = sb("nxtf", [P, 1])
        ea = sb("ea", [P, COLS])
        fmax = sb("fmax", [P, COLS + 1])
        s1 = sb("s1", [P, COLS])
        pen = sb("pen", [P, COLS + 1])
        same = sb("same", [P, COLS + 1])
        isfirst = sb("isfirst", [P, COLS])
        firstrow = sb("firstrow", [P, 4], i32)
        scat = sb("scat", [P, COLS], i32)
        xt = sb("xt", [P, GROUPS, E1, GC])
        idx = [sb(f"idx{b}", [P, 2, GC], i32) for b in range(2)]
        xs = [sb(f"xs{b}", [P, GC, D]) for b in range(2)]
        xd = [sb(f"xd{b}", [P, GC, D]) for b in range(2)]
        xsT = [sb(f"xsT{b}", [P, H, P]) for b in range(2)]
        xin = [sb(f"xin{b}", [P, JM, D]) for b in range(2)]
        yb = [sb(f"yb{b}", [P, JM, D]) for b in range(2)]
        flag = sb("flag", [P, 2])
        flagi = sb("flagi", [P, 1], i32)
        numbers = sb("numbers", [P, 4, GC], i32)
        rec = sb("rec", [P, GC, WORDS], i32)
        reci = sb("reci", [P, GC], i32)
        work = sb("work", [P, GC, D])
        sq = sb("sq", [P, JM, D])
        sq2 = sb("sq2", [P, 2 * GC, D])
        st = sb("st", [P, 4, JM])
        st2 = [sb(f"st2{b}", [P, 4, GC]) for b in range(2)]
        score = sb("score", [P, GC])
        shift = sb("shift", [P, GC])
        down = [sb(f"down{b}", [P, 2, GC]) for b in range(2)]
        decay = sb("decay", [P, E1, GC])
        prev = sb("prev", [P, E1])
        ends = sb("ends", [P, 2, P])
        brought = sb("brought", [P, 1])
        pull = ends[:, 0, :]
        carry = sb("carry", [P, E1])
        own = sb("own", [P, E1])
        pick = sb("pick", [P, GC])
        few = sb("few", [P, 8])
        zero = sb("zero", [P, 1])

        psT = [ctx.enter_context(nc.psum_tensor(f"psT{b}", [P, 2, 512], f32)) for b in range(2)]
        psX = [ctx.enter_context(nc.psum_tensor(f"psX{b}", [P, 2, 512], f32)) for b in range(2)]

        s_const = sem("s_const")
        s_ones = sem("s_ones")
        s_pads = sem("s_pads")
        s_apad = sem("s_apad")
        s_load = sem("s_load")
        s_bad = sem("s_bad")
        s_badp = sem("s_badp")
        s_flag = sem("s_flag")
        s_iota = sem("s_iota")
        s_row = sem("s_row")
        s_rowu = sem("s_rowu")
        s_rank = sem("s_rank")
        s_rec = sem("s_rec")
        s_rsc = sem("s_rsc")
        s_again = sem("s_again")
        s_edge = sem("s_edge")
        s_attr = sem("s_attr")
        s_alrep = sem("s_alrep")
        s_wps = sem("s_wps")
        s_wsb = sem("s_wsb")
        s_idx = pair("s_idx")
        s_gs = pair("s_gs")
        s_gd = pair("s_gd")
        s_tr = pair("s_tr")
        s_tc = pair("s_tc")
        s_xm = pair("s_xm")
        s_xc = pair("s_xc")
        s_er = pair("s_er")
        s_sp = pair("s_sp")
        s_xin = pair("s_xin")
        s_xu = pair("s_xu")
        s_yc = pair("s_yc")
        s_sq = pair("s_sq")
        s_y = pair("s_y")
        s_st = pair("s_st")
        s_var = pair("s_var")
        s_dev = pair("s_dev")
        s_bv = sem("s_bv")
        s_bd = sem("s_bd")
        s_v = sem("s_v")
        s_dn = pair("s_dn")
        s_w = pair("s_w")
        s_dc = pair("s_dc")
        s_ends = sem("s_ends")
        s_endp = sem("s_endp")
        s_farr = sem("s_farr")
        s_dia = sem("s_dia")
        s_spr = sem("s_spr")
        s_pl = sem("s_pl")
        s_ple = sem("s_ple")
        s_rch = sem("s_rch")
        s_cps = sem("s_cps")
        s_fc = sem("s_fc")
        s_fe = sem("s_fe")
        s_re = pair("s_re")
        s_all = sem("s_all")
        s_asq = pair("s_asq")
        s_b = pair("s_b")
        s_bsq = pair("s_bsq")
        s_av = pair("s_av")
        s_dump = sem("s_dump")
        s_fxd = sem("s_fxd")
        s_fown = sem("s_fown")
        s_fvar = sem("s_fvar")
        s_fdev = sem("s_fdev")
        s_fz = sem("s_fz")
        s_fsc = sem("s_fsc")
        s_ad = pair("s_ad")
        s_bvar = pair("s_bvar")
        s_bdev = pair("s_bdev")
        s_bi = pair("s_bi")
        s_z = [sem(f"s_z{q}") for q in range(4)]
        s_sc = [sem(f"s_sc{q}") for q in range(4)]

        attr = xt[:, :, :, :].rearrange("p g f c -> p (g f c)")[:, 0:COLS * DE].rearrange("p (c f) -> p c f", f=DE)

        STEPS_OF_ROUND = 32

        rooms = xt[:, :, :, :].rearrange("p g f c -> p (g f c)")[:, COLS * DE:COLS * DE + 5 * CH].rearrange(
            "p (k n) -> p k n", n=CH)
        rowi, place_i = rooms[:, 0, :].bitcast(i32), rooms[:, 3, :].bitcast(i32)
        rowf, place, less, tie = (rooms[:, k, :] for k in range(1, 5))

        def unsorted(eng):
            eng.wait_ge(s_flag, 1)
            return eng.If(eng.value_load(flagi[0:1, 0:1]) > 0)

        block = ctx.enter_context(nc.Block())

        class Steps:
            base, n = 0, 0

            def __call__(self, ins):
                ins.then_inc(s_v, 1)
                self.n += 1
                nc.vector.wait_ge(s_v, self.base + self.n)

        first_row = xin[1][:, JM - 1, :]
        found = xin[0][:, :, :].rearrange("p j f -> p (j f)")[:, 0:E1 * GC]

        def rows_of(q):
            return yb[q % 2][:, (q // 2) * GC:(q // 2 + 1) * GC, :]

        def numbers_of(q):
            return numbers[:, q, :]

        def square_a(b):
            return sq[:, b * GC:(b + 1) * GC, :]

        def square_b(b):
            return sq2[:, b * GC:(b + 1) * GC, :]

        def back_of(q, r):
            if q < 2 and isinstance(r, int) and r == 0:
                return xin[q][:, 0:GC, :]
            return xd[q % 2]

        def in_turn(eng, work_, after, before=None, step=None):
            def round_of_four(r, todo=range(4), last=False):
                for q in todo:
                    if before and not (last and q == 3):
                        before((q + 1) % 4, r + (q + 1) // 4)
                    work_(q, r)
                    if q != todo[0] or q == 0:
                        after((q - 1) % 4, r + (q - 1) // 4)

            rounds = GROUPS // 4
            if before:
                before(3, 0)
            round_of_four(0, range(3, 4))
            if step:
                start, step.n = step.n, 0
            with eng.Fori(1, rounds - 1) as r:
                if step:
                    step.base = (r - 1) * STEPS_OF_ROUND + start
                round_of_four(r)
            if step:
                assert step.n == STEPS_OF_ROUND, step.n
                step.base, step.n = 0, start + (rounds - 2) * STEPS_OF_ROUND
            round_of_four(rounds - 1, last=True)
            after(3, rounds - 1)

        def wait_free(eng, s, count):
            if not (isinstance(count, int) and count == 0):
                eng.wait_ge(s, count)

        def sums_of(g):
            return xt[:, bass.ds(g, 1), :, :].rearrange("p g f c -> p c (g f)")

        def over(row, n, width=D):
            return row.unsqueeze(1).broadcast_to([row.shape[0], n, width])

        def along(cols, width=D):
            return cols.unsqueeze(2).broadcast_to([cols.shape[0], cols.shape[1], width])

        @block.sync
        def _(sp):
            def edges(to, a, s):
                with nc.allow_non_contiguous_dma(reason="sorted edges are loaded word by word"):
                    sp.dma_start(to[0:FULLP], a[0:FULLP * COLS].rearrange("(p c) ... -> p c ...", p=FULLP)
                                 ).then_inc(s, 16)
                    sp.dma_start(to[FULLP:P, 0:REST], a[FULLP * COLS:EDGES].rearrange("(p c) ... -> p c ...", p=1)
                                 ).then_inc(s, 16)

            def neighbours(a, s):
                with nc.allow_non_contiguous_dma(reason="one number for each partition"):
                    sp.dma_start(nxti[0:FULLP, :], a[COLS:EDGES:COLS, :]).then_inc(s, 16)

            sp.wait_ge(s_pads, 1)
            edges(dsti[:, :], dst, s_edge)
            neighbours(dst.unsqueeze(1), s_edge)
            sp.wait_ge(s_pads, 2)
            edges(srci[:, :], src, s_edge)
            for b in range(2):
                sp.dma_start(xin[b][:, 0:J, :], dense(x, b, False)).then_inc(s_xin[b], 16)
            sp.dma_start(w1[:, :], W1).then_inc(s_load, 16)
            for k in range(2):
                sp.dma_start(w2[:, k * D:(k + 1) * D], W2).then_inc(s_load, 16)
                sp.dma_start(w1d[:, k * D:(k + 1) * D], W1[:, 0:D]).then_inc(s_load, 16)
            with nc.allow_non_contiguous_dma(reason="one number for each partition"):
                sp.dma_start(al[:, :], att_l.unsqueeze(1)).then_inc(s_load, 16)
            for k, row in enumerate((att_r, bias, gamma, beta)):
                sp.dma_start(rows[:, k, :], row.unsqueeze(0).broadcast_to([P, D])).then_inc(s_load, 16)
            sp.wait_ge(s_apad, 1)
            edges(attr, edge_attr, s_attr)

            with unsorted(sp):
                def chunk(k):
                    sp.dma_start(rowi, dst[bass.ds(k * CH, CH)].unsqueeze(0).broadcast_to([P, CH])).then_inc(s_row, 16)

                chunk(0)
                with sp.Fori(1, CHUNKS) as k:
                    sp.wait_ge(s_rowu, k)
                    chunk(k)
                sp.wait_ge(s_rsc, 16 * COLS)
                edges(dsti[:, :], ranked[:, 1], s_again)
                neighbours(ranked[:, 1:2], s_again)
                edges(srci[:, :], ranked[:, 0], s_again)
                edges(attr.bitcast(i32), ranked[:, 2:WORDS], s_again)

            def dense_io(b, i, load=(P, J), store=(P, J)):
                if load:
                    sp.wait_ge(s_xu[b], i + 1)
                    sp.dma_start(xin[b][0:load[0], 0:load[1], :], dense(x, i * 2 + b + 2, load != (P, J))
                                 ).then_inc(s_xin[b], 16)
                sp.wait_ge(s_y[b], i + 1)
                sp.dma_start(dense(out, i * 2 + b, store != (P, J)), yb[b][0:store[0], 0:store[1], :]
                             ).then_inc(s_st[b], 16)

            def spilled(b, i):
                sp.wait_ge(s_er[b], i + 1)
                sp.dma_start(group(spill, i * 2 + b, GC * D), xd[b][:, :, :].rearrange("p c f -> p (c f)")
                             ).then_inc(s_sp[b], 16)

            pairs = GROUPS // 2
            for b in range(2):
                dense_io(b, 0)
            with sp.Fori(0, pairs - 3) as i:
                for b in range(2):
                    spilled(b, i)
                    dense_io(b, i + 1)
            for b in range(2):
                spilled(b, pairs - 3)
                dense_io(b, pairs - 2, load=(LP, LJ) if b else (P, J))
            for b in range(2):
                spilled(b, pairs - 2)
                dense_io(b, pairs - 1, load=None, store=(LP, LJ) if b else (P, J))

            def back(q, r, n):
                sp.dma_start(back_of(q, r)[:, :, :].rearrange("p c f -> p (c f)"), group(spill, n, GC * D)
                             ).then_inc(s_re[q % 2], 16)

            def dump(n):
                flat = xt[:, :, :, :].rearrange("p g f c -> p (g f c)")
                sp.dma_start(run_sums[:, :].rearrange("(p g) w -> p (g w)", p=P)[:, bass.ds(n * (E1 * GC), 2 * E1 * GC)],
                             flat[:, bass.ds(n * (E1 * GC), 2 * E1 * GC)]).then_inc(s_dump, 16)

            for b in range(2):
                sp.wait_ge(s_xu[b], pairs)
                sp.wait_ge(s_sp[b], 16)
                back(b, 0, b)
            for b in range(2):
                spilled(b, pairs - 1)
                sp.wait_ge(s_sp[b], 16 * pairs)
                back(2 + b, 0, 2 + b)
            sp.wait_ge(s_all, 1)
            dump(0)
            dump(2)
            with sp.Fori(1, pairs - 1) as i:
                for b in range(2):
                    sp.wait_ge(s_b[b], i + 1)
                    back(b, i, i * 2 + b + 2)
                dump(i * 2 + 2)
            sp.wait_ge(s_dump, 16 * pairs)
            for b in range(2):
                sp.wait_ge(s_st[b], 16 * pairs)

        @block.gpsimd
        def _(pool):
            nc.gpsimd.memset(dsti[:, REST:COLS], FAR)
            nc.gpsimd.memset(nxti[:, :], 2 * FAR).then_inc(s_pads, 1)
            nc.gpsimd.memset(srci[:, REST:COLS], 0).then_inc(s_pads, 1)
            nc.gpsimd.memset(ones[:, :], 1.0).then_inc(s_ones, 1)
            nc.gpsimd.memset(ident[:, :], 0.0)
            nc.gpsimd.memset(eps[:, :], EPS)
            nc.gpsimd.memset(zero[:, :], 0.0)
            nc.gpsimd.iota(firstrow[:, 0:1], pattern=[[0, 1]], base=0, channel_multiplier=GROUPS)
            nc.gpsimd.memset(centre[:, :], -1.0 / D).then_inc(s_const, 1)
            pool.wait_ge(s_const, 1)
            nc.gpsimd.affine_select(out=ident[:, :], in_=ident[:, :], compare_op=ALU.not_equal, fill=1.0,
                                    base=0, pattern=[[1, P]], channel_multiplier=-1)
            nc.gpsimd.affine_select(out=reach[:, :], in_=ones[:, :], compare_op=ALU.is_gt, fill=0.0,
                                    base=0, pattern=[[1, P]], channel_multiplier=-1)
            nc.gpsimd.affine_select(out=far[:, :], in_=ones[:, :], compare_op=ALU.is_gt, fill=0.0,
                                    base=0, pattern=[[-1, P]], channel_multiplier=1)
            nc.gpsimd.affine_select(out=centre[:, :], in_=centre[:, :], compare_op=ALU.not_equal, fill=1.0 - 1.0 / D,
                                    base=0, pattern=[[1, D]], channel_multiplier=-1).then_inc(s_const, 1)

            with unsorted(pool):
                nc.gpsimd.iota(ea[:, :].bitcast(i32), pattern=[[1, COLS]], base=0, channel_multiplier=COLS)
                nc.gpsimd.iota(place_i, pattern=[[1, CH]], base=0, channel_multiplier=0).then_inc(s_iota, 1)
                pool.wait_ge(s_attr, 32)
                pool.wait_ge(s_rank, 1)
                with pool.Fori(0, GROUPS) as g:
                    now, out_ = pool.to_reg(g + 1), pool.to_reg(g * (16 * GC) + 16 * GC)
                    nc.gpsimd.tensor_copy(rec[:, :, 0], group(srci, g))
                    nc.gpsimd.tensor_copy(rec[:, :, 1], group(dsti, g))
                    nc.gpsimd.tensor_copy(rec[:, :, 2:WORDS], attr[:, bass.ds(g * GC, GC), :].bitcast(i32))
                    nc.gpsimd.tensor_copy(reci[:, :], group(scat, g)).then_inc(s_rec, 1)
                    pool.wait_ge(s_const, 1)
                    pool.wait_ge(s_rec, now)
                    for k in range(GC):
                        nc.gpsimd.indirect_dma_start(ranked[:, :], bass.IndirectOffsetOnAxis(
                            ap=reci[:, k:k + 1], axis=0), rec[:, k, :], None,
                            bounds_check=EDGES - 1, oob_is_err=False).then_inc(s_rsc, 16)
                    pool.wait_ge(s_const, 1)
                    pool.wait_ge(s_rsc, out_)

            def gathers(i):
                first = isinstance(i, int)
                before, after, spilled = (i, i + 1, i * 16) if first else (
                    i, pool.to_reg(i + 1), pool.to_reg(i * 16))
                for b in range(2):
                    pool.wait_ge(s_const, 1)
                    pool.wait_ge(s_idx[b], after)
                    wait_free(pool, s_tr[b], before)
                    for k in range(GC):
                        nc.gpsimd.indirect_dma_start(xs[b][:, k, :], None, x[:, :], bass.IndirectOffsetOnAxis(
                            ap=idx[b][:, 0, k:k + 1], axis=0)).then_inc(s_gs[b], 16)
                    pool.wait_ge(s_const, 1)
                    wait_free(pool, s_sp[b], spilled)
                    for k in range(GC):
                        nc.gpsimd.indirect_dma_start(xd[b][:, k, :], None, x[:, :], bass.IndirectOffsetOnAxis(
                            ap=idx[b][:, 1, k:k + 1], axis=0)).then_inc(s_gd[b], 16)

            gathers(0)
            with pool.Fori(1, GROUPS // 2) as i:
                gathers(i)

            for b in range(2):
                pool.wait_ge(s_st[b], 16 * (GROUPS // 2))
            nc.gpsimd.indirect_dma_start(first_row, None, x[:, :], bass.IndirectOffsetOnAxis(
                ap=dstg[:, 0:1], axis=0)).then_inc(s_fxd, 16)

            def scatters(r):
                after = r + 1 if isinstance(r, int) else pool.to_reg(r + 1)
                for q in range(4):
                    pool.wait_ge(s_const, 1)
                    pool.wait_ge(s_z[q], after)
                    for k in range(GC):
                        nc.gpsimd.indirect_dma_start(out[:, :], bass.IndirectOffsetOnAxis(
                            ap=numbers_of(q)[:, k:k + 1], axis=0), rows_of(q)[:, k, :], None,
                            bounds_check=NODES - 1, oob_is_err=False).then_inc(s_sc[q], 16)

            with pool.Fori(0, GROUPS // 4 - 1) as r:
                scatters(r)
            pool.wait_ge(s_dump, 16 * (GROUPS // 2))
            nc.gpsimd.indirect_dma_start(found, None, run_sums[:, :], bass.IndirectOffsetOnAxis(
                ap=firstrow[:, 1:2], axis=0)).then_inc(s_fown, 16)
            scatters(GROUPS // 4 - 1)
            pool.wait_ge(s_fz, 1)
            nc.gpsimd.indirect_dma_start(out[:, :], bass.IndirectOffsetOnAxis(ap=firstrow[:, 2:3], axis=0),
                                         first_row, None, bounds_check=NODES - 1, oob_is_err=False
                                         ).then_inc(s_fsc, 16)
            for q in range(4):
                pool.wait_ge(s_sc[q], 16 * GC * (GROUPS // 4))
            pool.wait_ge(s_fsc, 16)

        @block.scalar
        def _(act):
            def deviation(total, bias=eps):
                return nc.scalar.activation(total, total, ACT.Sqrt, scale=1.0 / D, bias=bias[0:total.shape[0], :])

            act.wait_ge(s_const, 1)
            act.wait_ge(s_bv, 1)
            deviation(sc[:, 1:2]).then_inc(s_bd, 1)

            def copies(b, i):
                act.wait_ge(s_tr[b], i + 1)
                wait_free(act, s_xm[b], i)
                nc.scalar.copy(xsT[b][:, 0:4, :].rearrange("p k e -> p (k e)"), psT[b][:, 0, :])
                nc.scalar.copy(xsT[b][:, 4:H, :].rearrange("p k e -> p (k e)"), psT[b][:, 1, 0:(H - 4) * P]
                               ).then_inc(s_tc[b], 1)

            def dense_part(b, i, np_=P, nj=J):
                act.wait_ge(s_yc[b], i + 1)
                nc.scalar.activation(sq[0:np_, 0:nj, :], yb[b][0:np_, 0:nj, :], ACT.Square).then_inc(s_sq[b], 1)
                act.wait_ge(s_var[b], i + 1)
                deviation(st[0:np_, 1, 0:nj]).then_inc(s_dev[b], 1)

            def weights(b, i):
                act.wait_ge(s_dn[b], i + 1)
                nc.scalar.activation(down[b][:, :, :], down[b][:, :, :], ACT.Exp).then_inc(s_w[b], 1)
                act.wait_ge(s_w[b], i + 1)
                nc.scalar.copy(decay[:, :, 1:GC], over(down[b][:, 0, 1:GC], E1, GC - 1)).then_inc(s_dc[b], 1)

            def part(i, end=(P, J)):
                for b in range(2):
                    copies(b, i)
                    weights(b, i)
                    dense_part(b, i + 1, *(end if b else (P, J)))

            def squares_of_sums(q, r):
                b, g = q % 2, r * 4 + q
                nc.scalar.activation(square_a(b), sums_of(g)[:, :, 0:D], ACT.Square).then_inc(s_asq[b], 1)

            def middle(q, r):
                b, i = q % 2, r * 2 + q // 2
                act.wait_ge(s_av[b], i + 1)
                deviation(st2[b][:, 1, :], zero).then_inc(s_ad[b], 1)
                act.wait_ge(s_b[b], i + 1)
                nc.scalar.activation(square_b(b), rows_of(q), ACT.Square).then_inc(s_bsq[b], 1)

            def scaled(q, r):
                b, i = q % 2, r * 2 + q // 2
                act.wait_ge(s_bvar[b], i + 1)
                deviation(st2[b][:, 3, :]).then_inc(s_bdev[b], 1)
                act.wait_ge(s_bi[b], i + 1)
                for k in range(GC):
                    last_row = nc.scalar.mul(rows_of(q)[:, k, :], rows_of(q)[:, k, :], st2[b][:, 3, k:k + 1])
                last_row.then_inc(s_z[q], 1)

            pairs = GROUPS // 2
            for b in range(2):
                dense_part(b, 0)
            part(0)
            with act.Fori(1, pairs - 2) as i:
                part(i)
            part(pairs - 2, (LP, LJ))
            end = pairs - 1
            squares_of_sums(0, 0)
            squares_of_sums(1, 0)
            middle(0, 0)
            scaled(0, 0)
            copies(0, end)
            middle(1, 0)
            scaled(1, 0)
            weights(0, end)
            copies(1, end)
            squares_of_sums(2, 0)
            middle(2, 0)
            scaled(2, 0)
            weights(1, end)
            act.wait_ge(s_all, 1)
            in_turn(act, middle, scaled, before=squares_of_sums)

            act.wait_ge(s_pl, 1)
            nc.scalar.activation(pull, pull, ACT.Exp).then_inc(s_ple, 1)
            act.wait_ge(s_fc, 1)
            nc.scalar.activation(few[:, 0:2], few[:, 0:2], ACT.Exp).then_inc(s_fe, 1)
            for k, bias_ in enumerate((zero, eps)):
                act.wait_ge(s_fvar, k + 1)
                deviation(few[:, 3:4], bias_).then_inc(s_fdev, 1)

        @block.tensor
        def _(pe):
            pe.wait_ge(s_ones, 1)
            pe.wait_ge(s_bad, 1)
            nc.tensor.matmul(psT[1][:, 1, 0:1], ones[:, :], flag[:, 0:1], start=True, stop=True).then_inc(s_badp, 1)
            pe.wait_ge(s_load, 16 * 10)
            pe.wait_ge(s_alrep, 1)
            nc.tensor.matmul(psT[0][:, 0, 0:D + DE], alrep[:, :], w1[:, :], start=True, stop=True)
            nc.tensor.matmul(psT[0][:, 1, 0:D], w2[:, :], centre[:, :], start=True, stop=True)
            nc.tensor.matmul(psT[1][:, 0, 0:1], w1d[:, :], al[:, :], start=True, stop=True).then_inc(s_wps, 1)
            pe.wait_ge(s_wsb, 1)
            pe.wait_ge(s_ends, 1)
            nc.tensor.matmul(psX[0][:, 0, 0:2 * P], ones[:, :], ends[:, :, :].rearrange("p k q -> p (k q)"),
                             start=True, stop=True).then_inc(s_endp, 1)
            pe.wait_ge(s_farr, 1)

            def products(i):
                for b in range(2):
                    pe.wait_ge(s_gs[b], i * (16 * GC) + 16 * GC)
                    wait_free(pe, s_tc[b], i)
                    for k in range(H):
                        last = nc.tensor.transpose(psT[b][:, k // 4, (k % 4) * P:(k % 4 + 1) * P],
                                                   xs[b][:, 2 * k:2 * k + 2, :].rearrange("p c f -> p (c f)"),
                                                   ident[:, :])
                    last.then_inc(s_tr[b], 1)
                    pe.wait_ge(s_tc[b], i + 1)
                    wait_free(pe, s_xc[b], i)
                    for h in range(2):
                        half = slice(D * h, D * (h + 1))
                        nc.tensor.matmul(psX[b][:, h, 0:H * E1], ones[half, :],
                                         brep[half, :, :].rearrange("p c f -> p (c f)"), start=True, stop=False)
                        for k in range(H):
                            last = nc.tensor.matmul(psX[b][:, h, k * E1:(k + 1) * E1], xsT[b][half, k, :],
                                                    wc[half, :], start=False, stop=(k == H - 1))
                    last.then_inc(s_xm[b], 1)

            products(0)
            with pe.Fori(1, GROUPS // 2) as i:
                products(i)
            for b in range(2):
                pe.wait_ge(s_tc[b], GROUPS // 2)
            for k in range(2):
                pe.wait_ge(s_dia, k + 1)
                nc.tensor.matmul(psT[k][:, 0, 0:P], ones[:, :], ends[:, k, :], start=True, stop=True).then_inc(s_spr, 1)
            pe.wait_ge(s_xc[0], GROUPS // 2)
            pe.wait_ge(s_rch, 1)
            nc.tensor.matmul(psX[0][:, 0, 0:E1], pull, prev[:, :], start=True, stop=True).then_inc(s_cps, 1)

        @block.vector
        def _(dve):
            V = nc.vector
            step = Steps()

            def done(ins, s, count):
                ins.then_inc(s, 1)
                dve.wait_ge(s, count)

            def copy_idx(g, b):
                V.tensor_copy(idx[b][:, 0, :], group(srci, g))
                V.tensor_copy(idx[b][:, 1, :], group(dstg, g)).then_inc(s_idx[b], 1)

            V.memset(attr[:, REST:COLS, :], 0.0).then_inc(s_apad, 1)
            dfirst, dlast = dstf[:, 0:1], dstf[:, COLS - 1:COLS]
            dve.wait_ge(s_edge, 16 * 5)
            V.tensor_copy(nxtf[:, :], nxti[:, :])
            step(V.tensor_copy(dstf[:, :], dsti[:, :]))
            V.tensor_tensor(same[:, 0:COLS - 1], dstf[:, 1:COLS], dstf[:, 0:COLS - 1], ALU.is_lt)
            step(V.tensor_tensor(same[:, COLS - 1:COLS], nxtf[:, :], dlast, ALU.is_lt))
            V.tensor_reduce(flag[:, 0:1], same[:, 0:COLS], AX, ALU.add).then_inc(s_bad, 1)
            dve.wait_ge(s_badp, 1)
            V.tensor_copy(flagi[:, :], psT[1][:, 1, 0:1]).then_inc(s_flag, 1)

            with unsorted(dve):
                def then(ins):
                    dve.drain()

                rank = fmax[:, 0:COLS]
                dve.wait_ge(s_iota, 1)
                V.tensor_copy(place, place_i)
                then(V.tensor_copy(s1[:, :], ea[:, :].bitcast(i32)))
                then(V.memset(rank, 0.0))
                with dve.Fori(0, CHUNKS) as k:
                    dve.wait_ge(s_row, k * 16 + 16)
                    V.tensor_copy(rowf, rowi).then_inc(s_rowu, 1)
                    dve.drain()
                    with dve.Fori(0, COLS) as c:
                        mine = dstf[:, bass.ds(c, 1)]
                        V.tensor_scalar(less, rowf, mine, None, ALU.is_lt)
                        then(V.tensor_scalar(tie, place, s1[:, bass.ds(c, 1)], None, ALU.is_lt))
                        then(V.scalar_tensor_tensor(tie, rowf, mine, tie, ALU.is_equal, ALU.mult))
                        then(V.tensor_tensor(less, less, tie, ALU.add))
                        then(V.tensor_reduce(flag[:, 1:2], less, AX, ALU.add))
                        then(V.tensor_tensor(rank[:, bass.ds(c, 1)], rank[:, bass.ds(c, 1)], flag[:, 1:2], ALU.add))
                    then(V.tensor_scalar(s1[:, :], s1[:, :], float(CH), None, ALU.subtract))
                V.tensor_copy(scat[:, :], rank).then_inc(s_rank, 1)
                dve.wait_ge(s_again, 16 * 7)
                V.tensor_copy(nxtf[:, :], nxti[:, :])
                then(V.tensor_copy(dstf[:, :], dsti[:, :]))

            step(V.scalar_tensor_tensor(dstg[:, :], dstf[:, :], float(FAR), dstf[:, :], ALU.is_lt, ALU.mult))
            for b in range(2):
                copy_idx(b, b)
            dve.wait_ge(s_load, 16 * 10)
            dve.wait_ge(s_const, 2)
            V.tensor_copy(alrep[:, :], al[:, 0:1].broadcast_to([D, P])).then_inc(s_alrep, 1)
            step(V.tensor_reduce(sc[:, 0:1], brow, AX, ALU.add))
            step(V.tensor_scalar(sc[:, 0:1], sc[:, 0:1], 1.0 / D, None, ALU.mult))
            step(V.tensor_scalar(brow, brow, sc[:, 0:1], None, ALU.subtract))
            step(V.tensor_tensor(crow[:, :], brow, brow, ALU.mult))
            V.tensor_reduce(sc[:, 1:2], crow[:, :], AX, ALU.add).then_inc(s_bv, 1)
            dve.wait_ge(s_bd, 1)
            step(V.reciprocal(sc[:, 2:3], sc[:, 1:2]))
            step(V.tensor_scalar(crow[:, :], brow, sc[:, 2:3], None, ALU.mult))
            step(V.tensor_tensor(crow[:, :], crow[:, :], grow, ALU.mult))
            step(V.tensor_tensor(crow[:, :], crow[:, :], erow, ALU.add))
            step(V.memset(brep[:, :, :], 0.0))
            step(V.tensor_scalar(brep[:, :, 0:D], over(brow, H), 1.0 / D, None, ALU.mult))
            dve.wait_ge(s_wps, 1)
            step(V.tensor_copy(vrow[:, :], psT[0][:, 0, 0:D + DE]))
            step(V.tensor_copy(wc[:, 0:D], psT[0][:, 1, 0:D]))
            done(V.tensor_copy(wc[:, D:E1], psT[1][:, 0, 0:1]), s_wsb, 1)
            dve.wait_ge(s_attr, 32)
            step(V.tensor_tensor(attr, attr, over(vrow[:, D:D + DE], COLS, DE), ALU.mult))
            step(V.tensor_reduce(ea[:, :], attr, AX, ALU.add))

            step(V.memset(same[:, 0:1], 0.0))
            V.tensor_tensor(same[:, 1:COLS], dstf[:, 1:COLS], dstf[:, 0:COLS - 1], ALU.is_equal)
            step(V.tensor_tensor(same[:, COLS:COLS + 1], dlast, nxtf[:, :], ALU.is_equal))
            V.tensor_scalar(pen[:, :], same[:, :], 1.0, BIG, ALU.subtract, ALU.mult)
            V.tensor_scalar(isfirst[:, :], dstf[:, :], dfirst, None, ALU.is_equal)
            V.memset(decay[:, :, 0:1], 0.0)
            V.memset(prev[:, :], 0.0)
            V.memset(fmax[:, 0:1], -BIG)
            step(V.scalar_tensor_tensor(s1[:, :], same[:, 1:COLS + 1], float(FAR), dstf[:, :], ALU.mult, ALU.add))
            V.tensor_tensor(few[:, 2:3], isfirst[:, COLS - 1:COLS], same[:, COLS:COLS + 1], ALU.mult)
            V.tensor_copy(few[:, 0:1], firstrow[:, 0:1])
            step(V.tensor_reduce(few[:, 1:2], isfirst[:, :].rearrange("p (g c) -> p g c", c=GC)[:, 1:GROUPS, 0],
                                 AX, ALU.add))
            step(V.tensor_tensor(few[:, 0:1], few[:, 0:1], few[:, 1:2], ALU.add))
            V.tensor_copy(firstrow[:, 1:2], few[:, 0:1])
            step(V.scalar_tensor_tensor(few[:, 2:3], few[:, 2:3], float(FAR), dfirst, ALU.mult, ALU.add))
            V.tensor_copy(firstrow[:, 2:3], few[:, 2:3])
            step(V.scalar_tensor_tensor(s1[:, :], isfirst[:, :], float(FAR), s1[:, :], ALU.mult, ALU.add))
            V.tensor_copy(scat[:, :], s1[:, :])
            for k, end in enumerate((dfirst, dlast)):
                ins = V.tensor_scalar(ends[:, k, :], ident[:, :], end, None, ALU.mult)
            ins.then_inc(s_ends, 1)
            dve.wait_ge(s_endp, 1)
            spread = psX[0][:, 0, 0:2 * P].rearrange("p (k q) -> p k q", q=P)
            step(V.scalar_tensor_tensor(reach[:, :], spread[:, 0, :], dlast, reach[:, :], ALU.is_equal, ALU.mult))
            step(V.scalar_tensor_tensor(far[:, :], spread[:, 1, :], dfirst, far[:, :], ALU.is_equal, ALU.mult))
            done(V.tensor_scalar(far[:, :], far[:, :], 1.0, BIG, ALU.subtract, ALU.mult), s_farr, 1)

            def dense_part(b, i, np_=P, nj=J):
                y, q, t = yb[b][0:np_, 0:nj, :], sq[0:np_, 0:nj, :], st[0:np_, :, 0:nj]
                dve.wait_ge(s_xin[b], i * 16 + 16)
                wait_free(dve, s_st[b], i * 16)
                done(V.tensor_tensor(y, xin[b][0:np_, 0:nj, :], over(crow[0:np_, :], nj), ALU.add), s_xu[b], i + 1)
                step(V.tensor_reduce(t[:, 0, :], y, AX, ALU.add))
                step(V.tensor_scalar(t[:, 0, :], t[:, 0, :], 1.0 / D, None, ALU.mult))
                done(V.tensor_tensor(y, y, along(t[:, 0, :]), ALU.subtract), s_yc[b], i + 1)
                dve.wait_ge(s_sq[b], i + 1)
                V.tensor_reduce(t[:, 1, :], q, AX, ALU.add).then_inc(s_var[b], 1)
                dve.wait_ge(s_dev[b], i + 1)
                step(V.reciprocal(t[:, 1, :], t[:, 1, :]))
                V.tensor_tensor(y, y, along(t[:, 1, :]), ALU.mult).then_inc(s_y[b], 1)

            def edge_part(b, i, last=False):
                g = i * 2 + b
                dve.wait_ge(s_gs[b], i * (16 * GC) + 16 * GC)
                dve.wait_ge(s_gd[b], i * (16 * GC) + 16 * GC)
                if not last:
                    copy_idx(g + 2, b)
                step(V.tensor_tensor(work[:, :, :], xd[b][:, :, :], over(arow, GC), ALU.mult))
                step(V.tensor_reduce(score[:, :], work[:, :, :], AX, ALU.add))
                V.tensor_tensor(xd[b][:, :, :], xd[b][:, :, :], over(erow, GC), ALU.add).then_inc(s_er[b], 1)
                step(V.tensor_tensor(score[:, :], score[:, :], group(ea, g), ALU.add))
                dve.wait_ge(s_xm[b], i + 1)
                product = psX[b][:, :, 0:H * E1].rearrange("p h (k f) -> p h k f", f=E1)
                by_bank = "p (k h) -> p h k"
                halves = score[:, :].rearrange(by_bank, h=2)
                step(V.tensor_tensor(halves, halves, product[:, :, :, D], ALU.add))
                step(V.scalar_tensor_tensor(score[:, :], score[:, :], SLOPE, score[:, :], ALU.mult, ALU.max))
                before, now = group(fmax, g), fmax[:, bass.ds(g * GC + 1, GC)]
                step(V.tensor_tensor_scan(now, group(pen, g), score[:, :], before[:, 0:1], ALU.add, ALU.max))
                V.tensor_tensor(down[b][:, 1, :], score[:, :], now, ALU.subtract)
                step(V.tensor_tensor(shift[:, :], before, group(pen, g), ALU.add))
                V.tensor_tensor(down[b][:, 0, :], shift[:, :], now, ALU.subtract).then_inc(s_dn[b], 1)
                dve.wait_ge(s_w[b], i + 1)
                rows_ = xt[:, bass.ds(g, 1), :, :].rearrange("p g f c -> p (g f) c")
                V.tensor_copy(rows_[:, D, :], down[b][:, 1, :])
                into = rows_[:, 0:D, :].rearrange("p f (k h) -> p h k f", h=2)
                weight = down[b][:, 1, :].rearrange(by_bank, h=2)
                for h in range(2):
                    ins = V.tensor_tensor(into[:, h], product[:, h, :, 0:D], along(weight[:, h, :]), ALU.mult)
                done(ins, s_xc[b], i + 1)
                step(V.scalar_tensor_tensor(rows_[:, :, 0], prev[:, :], down[b][:, 0, 0:1], rows_[:, :, 0],
                                            ALU.mult, ALU.add))
                dve.wait_ge(s_dc[b], i + 1)
                flat = rows_.rearrange("p f c -> p (f c)")
                step(V.tensor_tensor_scan(flat, decay[:, :, :].rearrange("p f c -> p (f c)"), flat, 0.0,
                                          ALU.mult, ALU.add))
                step(V.tensor_copy(prev[:, :], rows_[:, :, GC - 1]))

            def repeat(count, body):
                start = step.n
                body(0)
                assert step.n == start + PER[body.__name__], (body.__name__, step.n - start)
                with dve.Fori(1, count) as i:
                    step.base, step.n = i * PER[body.__name__] + start, 0
                    body(i)
                step.base, step.n = 0, start + count * PER[body.__name__]

            PER = {"pair_of_groups": 2 * 13}

            def pair_of_groups(i, end=(P, J)):
                for b in range(2):
                    edge_part(b, i)
                    dense_part(b, i + 1, *(end if b else (P, J)))

            for b in range(2):
                dense_part(b, 0)
            pairs = GROUPS // 2
            repeat(pairs - 2, pair_of_groups)
            pair_of_groups(pairs - 2, (LP, LJ))

            def rows_out(q, r):
                b, i, g = q % 2, r * 2 + q // 2, r * 4 + q
                y, sums = rows_of(q), sums_of(g)
                den, rs, mu, _ = (st2[b][:, k, :] for k in range(4))
                step(V.scalar_tensor_tensor(den, sums[:, :, D], EPS * D, sums[:, :, D], ALU.mult, ALU.mult))
                dve.wait_ge(s_asq[b], i + 1)
                step(V.tensor_reduce(rs, square_a(b), AX, ALU.add))
                V.tensor_tensor(rs, rs, den, ALU.add).then_inc(s_av[b], 1)
                wait_free(dve, s_sc[q], r * (16 * GC))
                V.tensor_copy(numbers_of(q), group(scat, g))
                dve.wait_ge(s_ad[b], i + 1)
                step(V.reciprocal(rs, rs))
                step(V.tensor_tensor(y, sums[:, :, 0:D], along(rs), ALU.mult))
                step(V.tensor_tensor(y, y, over(grow, GC), ALU.mult))
                dve.wait_ge(s_re[b], i * 16 + 16)
                step(V.tensor_tensor(y, y, back_of(q, r)[:, :, :], ALU.add))
                step(V.tensor_reduce(mu, y, AX, ALU.add))
                step(V.tensor_scalar(mu, mu, 1.0 / D, None, ALU.mult))
                V.tensor_tensor(y, y, along(mu), ALU.subtract).then_inc(s_b[b], 1)

            def variances(q, r):
                b, i = q % 2, r * 2 + q // 2
                dv = st2[b][:, 3, :]
                dve.wait_ge(s_bsq[b], i + 1)
                V.tensor_reduce(dv, square_b(b), AX, ALU.add).then_inc(s_bvar[b], 1)
                dve.wait_ge(s_bdev[b], i + 1)
                V.reciprocal(dv, dv).then_inc(s_bi[b], 1)

            end = pairs - 1
            for q in range(2):
                dve.wait_ge(s_st[q], 16 * (end + 1))
                rows_out(q, 0)
                variances(q, 0)
            edge_part(0, end, True)
            rows_out(2, 0)
            variances(2, 0)
            edge_part(1, end, True)
            V.tensor_copy(few[:, 4:5], prev[:, D:E1]).then_inc(s_all, 1)
            in_turn(dve, rows_out, variances, step=step)

            for k, end in enumerate((fmax[:, COLS:COLS + 1], brought[:, :])):
                if k == 1:
                    step(V.tensor_tensor(far[:, :], psT[0][:, 0, 0:P], far[:, :], ALU.add))
                    step(V.tensor_reduce(brought[:, :], far[:, :], AX, ALU.max))
                V.tensor_scalar(ends[:, k, :], ident[:, :], end, None, ALU.mult).then_inc(s_dia, 1)
                dve.wait_ge(s_spr, k + 1)
            step(V.tensor_scalar(pull, psT[1][:, 0, 0:P], -1.0, fmax[:, COLS:COLS + 1], ALU.mult, ALU.add))
            V.tensor_scalar(pull, pull, 0.0, None, ALU.min).then_inc(s_pl, 1)
            dve.wait_ge(s_ple, 1)
            done(V.tensor_tensor(pull, pull, reach[:, :], ALU.mult), s_rch, 1)
            at, top = s1[:, :], few[:, 2:3]
            V.tensor_tensor(at[:, 0:COLS - 1], isfirst[:, 0:COLS - 1], isfirst[:, 1:COLS], ALU.subtract)
            step(V.tensor_copy(at[:, COLS - 1:COLS], isfirst[:, COLS - 1:COLS]))
            V.tensor_reduce(pick[:, :], at.rearrange("p (g c) -> p c g", c=GC), AX, ALU.add)
            step(V.tensor_tensor(ea[:, :], at, fmax[:, 1:COLS + 1], ALU.mult))
            step(V.tensor_reduce(few[:, 0:1], ea[:, :], AX, ALU.add))
            step(V.tensor_tensor(top, few[:, 0:1], brought[:, :], ALU.max))
            V.tensor_tensor(few[:, 1:2], brought[:, :], top, ALU.subtract)
            V.tensor_tensor(few[:, 0:1], few[:, 0:1], top, ALU.subtract).then_inc(s_fc, 1)
            dve.wait_ge(s_cps, 1)
            V.tensor_copy(carry[:, :], psX[0][:, 0, 0:E1])

            dve.wait_ge(s_fown, 16)
            step(V.tensor_tensor(decay[:, :, :], found.rearrange("p (f c) -> p f c", c=GC), over(pick[:, :], E1, GC),
                                 ALU.mult))
            step(V.tensor_reduce(own[:, :], decay[:, :, :], AX, ALU.add))
            dve.wait_ge(s_fe, 1)
            step(V.tensor_scalar(own[:, :], own[:, :], few[:, 0:1], None, ALU.mult))
            step(V.scalar_tensor_tensor(own[:, :], carry[:, :], few[:, 1:2], own[:, :], ALU.mult, ALU.add))
            row, total, squares, y = own[:, 0:D], few[:, 3:4], work[:, 0, :], first_row
            V.scalar_tensor_tensor(few[:, 2:3], own[:, D:E1], EPS * D, own[:, D:E1], ALU.mult, ALU.mult)
            step(V.tensor_tensor(squares, row, row, ALU.mult))
            step(V.tensor_reduce(total, squares, AX, ALU.add))
            V.tensor_tensor(total, total, few[:, 2:3], ALU.add).then_inc(s_fvar, 1)
            dve.wait_ge(s_fdev, 1)
            step(V.reciprocal(total, total))
            step(V.tensor_scalar(row, row, total, None, ALU.mult))
            step(V.tensor_tensor(row, row, grow, ALU.mult))
            step(V.tensor_tensor(row, row, erow, ALU.add))
            dve.wait_ge(s_fxd, 16)
            step(V.tensor_tensor(y, y, row, ALU.add))
            step(V.tensor_reduce(few[:, 5:6], y, AX, ALU.add))
            step(V.tensor_scalar(few[:, 5:6], few[:, 5:6], 1.0 / D, None, ALU.mult))
            step(V.tensor_scalar(y, y, few[:, 5:6], None, ALU.subtract))
            step(V.tensor_tensor(squares, y, y, ALU.mult))
            V.tensor_reduce(total, squares, AX, ALU.add).then_inc(s_fvar, 1)
            dve.wait_ge(s_fdev, 2)
            step(V.reciprocal(total, total))
            V.tensor_scalar(y, y, total, None, ALU.mult).then_inc(s_fz, 1)


def kernel(**inputs):
    import numpy as _np
    import concourse.bacc as _bacc
    from concourse import mybir as _mybir
    from concourse.bass_utils import run_bass_kernel_spmd as _run

    nc = _bacc.Bacc("TRN2", target_bir_lowering=False, num_devices=1)
    arrays, args = {}, []
    for name in ("x", "src", "dst", "edge_attr_16", "L0_gnn_W1", "L0_gnn_W2", "L0_gnn_att_l", "L0_gnn_att_r",
                 "L0_gnn_bias", "L0_gnn_ln_gamma", "L0_gnn_ln_beta"):
        a = _np.ascontiguousarray(inputs[name])
        arrays[f"in_{name}_dram"] = a
        args.append(nc.dram_tensor(f"in_{name}_dram", a.shape, _mybir.dt.from_np(a.dtype), kind="ExternalInput").ap())
    args.append(nc.dram_tensor("out_0_dram", (100000, 64), _mybir.dt.float32, kind="ExternalOutput").ap())
    gnn_resnorm(nc, *args)
    r = _run(nc, [arrays], core_ids=[0])
    return r.results[0]["out_0_dram"]
```
